# Optimizing a Trainium2 kernel written in Bass

```python
import numpy as np
import jax
import jax.numpy as jnp

def _softmax(x, axis=-1):
    return jax.nn.softmax(x, axis=axis)

def _gelu(x):
    return jax.nn.gelu(x, approximate=True)

def _silu(x):
    return jax.nn.silu(x)

def _sigmoid(x):
    return jax.nn.sigmoid(x)

def _layernorm(x, axis=-1, eps=1e-05):
    m = jnp.mean(x, axis=axis, keepdims=True)
    v = jnp.var(x, axis=axis, keepdims=True)
    return (x - m) / jnp.sqrt(v + eps)

def _scatter_add(tgt, idx, src, axis=0):
    return tgt.at[idx].add(src)

def _segment_sum(src, seg, n):
    return jax.ops.segment_sum(src, seg, n)
kernel_name = 'mk_macaron_d1_jaxref_r4_58a9b8'

def setup_inputs(seed: int=0):
    np.random.seed(seed)
    _w = jnp.asarray

    def _L0_attn_setup():
        import jax, jax.numpy as jnp
        import numpy as np
        B, S, D, H = (4, 2048, 256, 16)
        DH = D // H
        key = jax.random.key(seed)
        ks = jax.random.split(key, 11)
        sc = 0.02
        return {'x': jax.random.normal(ks[0], (B, S, D), dtype=jnp.float32), 'Wp': jax.random.normal(ks[1], (D, D), dtype=jnp.float32) * sc, 'bp': jnp.zeros((D,), dtype=jnp.float32), 'Wq': jax.random.normal(ks[2], (D, D), dtype=jnp.float32) * sc, 'bq': jnp.zeros((D,), dtype=jnp.float32), 'Wk': jax.random.normal(ks[3], (D, D), dtype=jnp.float32) * sc, 'bk': jnp.zeros((D,), dtype=jnp.float32), 'Wv': jax.random.normal(ks[4], (D, D), dtype=jnp.float32) * sc, 'bv': jnp.zeros((D,), dtype=jnp.float32), 'Wo': jax.random.normal(ks[5], (D, D), dtype=jnp.float32) * sc, 'bo': jnp.zeros((D,), dtype=jnp.float32)}
    _L0_attn_in = _L0_attn_setup()

    def _L0_ffn_setup():
        import jax, jax.numpy as jnp
        import numpy as np
        B, S, D = (4, 512, 256)
        O = 256
        E = 8
        K = 2
        key = jax.random.key(seed)
        k1, k2, k3, k4, k5 = jax.random.split(key, 5)
        scale = 1.0 / np.sqrt(D)
        x = jax.random.normal(k1, (B, S, D), dtype=jnp.float32)
        We = jax.random.uniform(k2, (E, D, O), dtype=jnp.float32, minval=-scale, maxval=scale)
        be = jax.random.uniform(k3, (E, O), dtype=jnp.float32, minval=-scale, maxval=scale)
        Wg = jax.random.uniform(k4, (D, E), dtype=jnp.float32, minval=-scale, maxval=scale)
        bg = jax.random.uniform(k5, (E,), dtype=jnp.float32, minval=-scale, maxval=scale)
        return {'x': x, 'We': We, 'be': be, 'Wg': Wg, 'bg': bg}
    _L0_ffn_in = _L0_ffn_setup()
    _d = {'L0_attn_x': _L0_attn_in['x'], 'L0_attn_Wp': _L0_attn_in['Wp'], 'L0_attn_bp': _L0_attn_in['bp'], 'L0_attn_Wq': _L0_attn_in['Wq'], 'L0_attn_bq': _L0_attn_in['bq'], 'L0_attn_Wk': _L0_attn_in['Wk'], 'L0_attn_bk': _L0_attn_in['bk'], 'L0_attn_Wv': _L0_attn_in['Wv'], 'L0_attn_bv': _L0_attn_in['bv'], 'L0_attn_Wo': _L0_attn_in['Wo'], 'L0_attn_bo': _L0_attn_in['bo'], 'L0_ffn_We': _L0_ffn_in['We'], 'L0_ffn_be': _L0_ffn_in['be'], 'L0_ffn_Wg': _L0_ffn_in['Wg'], 'L0_ffn_bg': _L0_ffn_in['bg']}
    _x0 = _d['L0_attn_x']
    _d['L0_attn_x'] = jax.random.normal(jax.random.fold_in(jax.random.key(seed), 1), (4, 2048, 256), dtype=_x0.dtype)
    del _x0
    return _d

def reference(L0_attn_x, L0_attn_Wp, L0_attn_bp, L0_attn_Wq, L0_attn_bq, L0_attn_Wk, L0_attn_bk, L0_attn_Wv, L0_attn_bv, L0_attn_Wo, L0_attn_bo, L0_ffn_We, L0_ffn_be, L0_ffn_Wg, L0_ffn_bg):

    def _L0_attn_ref(x, Wp, bp, Wq, bq, Wk, bk, Wv, bv, Wo, bo):
        import jax, jax.numpy as jnp
        import numpy as np
        B, S, D, H = (4, 2048, 256, 16)
        DH = D // H
        b, s, d = x.shape
        scale = 1.0 / jnp.sqrt(jnp.asarray(DH, dtype=x.dtype))
        xp = x @ Wp.T + bp
        q = ((xp @ Wq.T + bq) * scale).reshape(b, s, H, DH)
        k = (xp @ Wk.T + bk).reshape(b, s, H, DH)
        v = (xp @ Wv.T + bv).reshape(b, s, H, DH)
        i = jnp.arange(s)
        idx = jnp.stack([(i - 1) % s, i, (i + 1) % s], axis=1)
        kn = k[:, idx]
        vn = v[:, idx]
        scores = jnp.einsum('bshd,bsnhd->bshn', q, kn)
        attn = jax.nn.softmax(scores, axis=-1)
        out = jnp.einsum('bshn,bsnhd->bshd', attn, vn).reshape(b, s, d)
        return out @ Wo.T + bo

    def _L0_ffn_ref(x, We, be, Wg, bg):
        import jax, jax.numpy as jnp
        import numpy as np
        B, S, D = (4, 512, 256)
        O = 256
        E = 8
        K = 2
        b, s, d = x.shape
        x_flat = x.reshape(-1, d)
        gates = jax.nn.softmax(x_flat @ Wg + bg, axis=-1)
        topk_gates, topk_idx = jax.lax.top_k(gates, K)
        topk_gates = topk_gates / jnp.sum(topk_gates, axis=1, keepdims=True)
        expert_out = jnp.einsum('nd,edo->neo', x_flat, We) + be
        selected = jnp.take_along_axis(expert_out, topk_idx[:, :, None], axis=1)
        out = jnp.sum(selected * topk_gates[:, :, None], axis=1)
        return out.reshape(b, s, -1)
    x = L0_attn_x
    x = x + 0.5 * _L0_ffn_ref(_layernorm(x, axis=-1), L0_ffn_We, L0_ffn_be, L0_ffn_Wg, L0_ffn_bg)
    x = x + _L0_attn_ref(_layernorm(x, axis=-1), L0_attn_Wp, L0_attn_bp, L0_attn_Wq, L0_attn_bq, L0_attn_Wk, L0_attn_bk, L0_attn_Wv, L0_attn_bv, L0_attn_Wo, L0_attn_bo)
    x = x + 0.5 * _L0_ffn_ref(_layernorm(x, axis=-1), L0_ffn_We, L0_ffn_be, L0_ffn_Wg, L0_ffn_bg)
    return x

_drawn_inputs = setup_inputs


def setup_inputs(seed=0):
    import zlib

    import numpy as np

    out = dict(_drawn_inputs(seed))
    spreads = {'L0_attn_bp': (0.0, 0.381),
     'L0_attn_bq': (0.0, 2.0),
     'L0_attn_bk': (0.0, 2.0),
     'L0_attn_bv': (0.0, 0.1),
     'L0_attn_bo': (0.0, 0.1)}
    factors = {'L0_attn_Wq': 22.068, 'L0_attn_Wk': 8.0}
    for name, (base, spread) in spreads.items():
        noise = np.random.default_rng([zlib.crc32(name.encode()), seed]).standard_normal(out[name].shape)
        drawn = base * np.exp(spread * noise) if base else spread * noise
        out[name] = jnp.asarray(drawn.astype(out[name].dtype))
    for name, factor in factors.items():
        out[name] = (out[name] * factor).astype(out[name].dtype)
    return out
```

```python
import concourse.bass as bass
from concourse import mybir
from contextlib import ExitStack

INPUTS = ["L0_attn_x", "L0_attn_Wp", "L0_attn_bp", "L0_attn_Wq", "L0_attn_bq", "L0_attn_Wk", "L0_attn_bk",
          "L0_attn_Wv", "L0_attn_bv", "L0_attn_Wo", "L0_attn_bo", "L0_ffn_We", "L0_ffn_be", "L0_ffn_Wg", "L0_ffn_bg"]
B, S, D, H, E = 4, 2048, 256, 16, 8
DH = D // H
PART = 128
TILES = B * S // PART
ROWS = S // TILES
KB = D // PART
PAIRS = TILES // 2 + 1
GROUPS = TILES // 2
BANK = 512
EPS = 1e-5
LOWEST_STEP, FIRST_FULL, LAST_FULL, LAST_STEP = -1, 7, 30, GROUPS + 3
GATE_OPS = 15
ATTN_OPS = 16
RESIDUAL_SUMS = 3


class Step:

    def __init__(self, const, reg=None):
        self.const, self.reg = const, reg

    def __add__(self, k):
        return Step(self.const + k, self.reg)

    def __sub__(self, k):
        return Step(self.const - k, self.reg)

    @property
    def slot(self):
        return self.const % 2

    def within(self, count):
        return self.reg is not None or 0 <= self.const < count

    def times(self, per, plus=0):
        value = per * self.const + plus
        return value if self.reg is None else self.reg * (2 * per) + value


def await_(eng, sem, value):
    if not isinstance(value, int) or value > 0:
        eng.wait_ge(sem, value)


def run_steps(eng, body, first_full=FIRST_FULL, last_full=LAST_FULL):
    for s in range(LOWEST_STEP, first_full):
        body(Step(s))
    with eng.Fori(0, (last_full + 1 - first_full) // 2) as i:
        for u in range(2):
            body(Step(first_full + u, i))
    for s in range(last_full + 1, LAST_STEP + 1):
        body(Step(s))


def build(nc, x, Wp, bp, Wq, bq, Wk, bk, Wv, bv, Wo, bo, We, be, Wg, bg, out):
    f32, f32r, u32 = mybir.dt.float32, mybir.dt.float32r, mybir.dt.uint32
    ACT, ALU, AX = mybir.ActivationFunctionType, mybir.AluOpType, mybir.AxisListType
    FFN1, FFN2 = 0, 1
    NF = 2
    LN1, LN2, LN3 = range(3)
    TA, TB, TO, TD = range(4)
    T_OF_LN = {LN1: TA, LN2: TB, LN3: TD}
    T_OF_FFN = {FFN1: TA, FFN2: TD}

    with ExitStack() as ctx:
        def sb(name, shape, dt=f32):
            return ctx.enter_context(nc.sbuf_tensor(name, shape, dt))

        def pb(name):
            return ctx.enter_context(nc.psum_tensor(name, [PART, BANK], f32))

        def sem(name):
            return ctx.enter_context(nc.semaphore(name))

        we_hi, we_lo = sb("we_hi", [PART, KB, E * D], f32r), sb("we_lo", [PART, KB, E * D], f32r)
        wqkv_hi, wqkv_lo = sb("wqkv_hi", [PART, KB, 3 * D], f32r), sb("wqkv_lo", [PART, KB, 3 * D], f32r)
        wo_hi, wo_lo = sb("wo_hi", [PART, KB, D], f32r), sb("wo_lo", [PART, KB, D], f32r)
        wg_hi, wg_lo = sb("wg_hi", [PART, KB, E], f32r), sb("wg_lo", [PART, KB, E], f32r)
        be_rows = sb("be_rows", [PART, 2, D], f32r)
        bqkv = sb("bqkv", [PART, 3 * D])
        bo_all = sb("bo_all", [PART, D])
        bg_all = sb("bg_all", [PART, 2, E])
        ident = sb("ident", [PART, PART])
        expert_no = sb("expert_no", [PART, 2, 2, E])
        idle = sb("idle", [PART, 2])
        minus_half, eps = sb("minus_half", [PART, 2]), sb("eps", [PART, 2])
        we_raw = sb("we_raw", [PART, KB, E * D])
        w_raw = sb("w_raw", [PART, 5, KB, D])
        wT, woT = sb("wT", [PART, KB, 3 * D]), sb("woT", [PART, KB, D])
        wg_raw = sb("wg_raw", [PART, KB, E])
        bp_col = sb("bp_col", [PART, KB])
        bp_wide, bv_wide = sb("bp_wide", [PART, KB, PART]), sb("bv_wide", [PART, KB, PART])
        be_raw, be_hi, be_lo = sb("be_raw", [PART, D]), sb("be_hi", [PART, D]), sb("be_lo", [PART, D])
        row_mask = sb("row_mask", [PART, 4])
        x_in = sb("x_in", [PART, 2, 2, D])
        stats = sb("stats", [PART, 3, 2, 6])
        mean_var = sb("mean_var", [PART, 3, 2, 2])
        var_eps, rstd = sb("var_eps", [PART, 3, 2]), sb("rstd", [PART, 3, 2])
        normed = sb("normed", [PART, 3, 2, D])
        T_hi = [sb(f"T_hi{i}", [PART, 2, KB, PART], f32r) for i in range(4)]
        T_lo = [sb(f"T_lo{i}", [PART, 2, KB, PART], f32r) for i in range(4)]
        logits = sb("logits", [PART, NF, 2, E])
        top = sb("top", [PART, NF, 2, 8])
        top_at = sb("top_at", [PART, NF, 2, 8], u32)
        top_no = sb("top_no", [PART, NF, 2, 2])
        margin, second = sb("margin", [PART, NF, 2]), sb("second", [PART, NF, 2])
        twice_sum = sb("twice_sum", [PART, NF, 2])
        share = sb("share", [PART, NF, 2, 2])
        hot = sb("hot", [PART, NF, 2, 2, E])
        hot_share = sb("hot_share", [PART, NF, 2, 2, E])
        gate = sb("gate", [PART, NF, 2, E])
        gate_parts = sb("gate_parts", [PART, NF, 4, 4, E])
        gateT = sb("gateT", [PART, NF, PART], f32r)
        bias_sum = sb("bias_sum", [PART, NF, 2, D])
        base = sb("base", [PART, NF, 2, D])
        scaled = we_raw[:].rearrange("p k (a b c n) -> p k a b c n", a=2, b=2, c=2)
        chain_sum = sb("chain_sum", [PART, NF, 2, 2, D])
        pool_sum = sb("pool_sum", [PART, NF, 2, D])
        x1 = sb("x1", [PART, 2, 2, D])
        x1_bo = sb("x1_bo", [PART, 4, D])
        qk = sb("qk", [PART, 4, 2, D])
        v = sb("v", [PART, 4, D])
        prod = sb("prod", [PART, 3, 2, D])
        score, prob = sb("score", [PART, 3, 2 * H]), sb("prob", [PART, 3, 2 * H])
        most = sb("most", [PART, 2, 2 * H])
        total = sb("total", [PART, 3, 2 * H])
        attn = sb("attn", [PART, 2, D])
        x2 = sb("x2", [PART, 2, 2, D])
        y = sb("y", [PART, 2, 2, D])

        ffn_bank = [pb(f"ffn_bank{b}") for b in range(4)]
        tr_bank = [pb(f"tr_bank{b}") for b in range(2)]
        mix_bank = [pb(f"mix_bank{b}") for b in range(2)]
        t_bank = {TO: tr_bank[0], TB: tr_bank[0], TA: tr_bank[1], TD: tr_bank[1]}
        gateT_bank = [mix_bank[0], tr_bank[0]]
        logit_bank = [tr_bank[1], mix_bank[1]]
        bias_bank = [mix_bank[1], mix_bank[0]]

        we_loaded, w_loaded, small_loaded = sem("we_loaded"), sem("w_loaded"), sem("small_loaded")
        be_zero, consts_set, masks_set, ident_set = sem("be_zero"), sem("consts_set"), sem("masks_set"), sem("ident_set")
        setup_act, setup_dve, setup_pe = sem("setup_act"), sem("setup_dve"), sem("setup_pe")
        edge_loaded = sem("edge_loaded")
        x_loaded = [sem(f"x_loaded{c}") for c in range(2)]
        y_stored = [sem(f"y_stored{c}") for c in range(2)]
        stat_done = [sem(f"stat_done{i}") for i in range(3)]
        rstd_done = [sem(f"rstd_done{i}") for i in range(3)]
        normed_done = [sem(f"normed_done{i}") for i in range(3)]
        T_done = [sem(f"T_done{i}") for i in range(4)]
        hi_done = [sem(f"hi_done{i}") for i in range(4)]
        lo_done = [sem(f"lo_done{i}") for i in range(4)]
        logits_done = [sem(f"logits_done{f}") for f in range(NF)]
        gate_ops = [sem(f"gate_ops{f}") for f in range(NF)]
        second_done = [sem(f"second_done{f}") for f in range(NF)]
        gateT_done = [sem(f"gateT_done{f}") for f in range(NF)]
        gateT_copied = [sem(f"gateT_copied{f}") for f in range(NF)]
        bias_done = [sem(f"bias_done{f}") for f in range(NF)]
        bias_copied = [sem(f"bias_copied{f}") for f in range(NF)]
        base_done = [sem(f"base_done{f}") for f in range(NF)]
        bank_full = [sem(f"bank_full{f}") for f in range(NF)]
        scaled_done = [sem(f"scaled_done{f}") for f in range(NF)]
        chain_done = [sem(f"chain_done{f}") for f in range(NF)]
        sum_done = [sem(f"sum_done{f}") for f in range(NF)]
        qk_done, v_done = sem("qk_done"), sem("v_done")
        qk_copied, v_copied = sem("qk_copied"), sem("v_copied")
        attn_ops, exp_done, proj_done, x2_done, x1_bo_done = (
            sem("attn_ops"), sem("exp_done"), sem("proj_done"), sem("x2_done"), sem("x1_bo_done"))

        block = ctx.enter_context(nc.Block())
        x_tiles = x.rearrange("b (r j) d -> (b r) j d", j=TILES)
        x_rows = x.rearrange("b (r j) d -> b r j d", j=TILES)
        out_tiles = out.rearrange("b (r j) d -> (b r) j d", j=TILES)

        @block.sync
        def _(sp):
            for w, W in enumerate((Wq, Wk, Wv, Wo, Wp)):
                sp.dma_start(w_raw[:, w, :, :], W.rearrange("(k p) n -> p k n", p=PART)).then_inc(w_loaded, 16)
            for b in range(B):
                sp.dma_start(x_in[ROWS * b + 1:ROWS * (b + 1), 0, 0, :],
                             x_rows[b, 0:ROWS - 1, TILES - 1, :]).then_inc(edge_loaded, 16)
            sp.dma_start(x_in[0:PART:ROWS, 0, 0, :], x_rows[:, ROWS - 1, TILES - 1, :]).then_inc(edge_loaded, 16)
            sp.dma_start(x_in[:, 0, 1, :], x_tiles[:, 0, :]).then_inc(edge_loaded, 16)
            sp.dma_start(x_in[:, 1, :, :], x_tiles[:, 1:3, :]).then_inc(x_loaded[1], 16)
            for k in range(KB):
                sp.dma_start(we_raw[:, k, :].rearrange("p (e n) -> p e n", e=E),
                             We[:, k * PART:(k + 1) * PART, :].rearrange("e p n -> p e n")).then_inc(we_loaded, 16)

            def body(s):
                n = s + 3
                if n.within(PAIRS):
                    await_(sp, base_done[FFN1], (s + 1).times(1, 1))
                    if n.reg is None and n.const == PAIRS - 1:
                        sp.dma_start(x_in[:, 0, 0, :], x_tiles[:, TILES - 1, :]).then_inc(edge_loaded, 16)
                        for b in range(B):
                            sp.dma_start(x_in[ROWS * b:ROWS * (b + 1) - 1, 0, 1, :],
                                         x_rows[b, 1:ROWS, 0, :]).then_inc(edge_loaded, 16)
                        sp.dma_start(x_in[ROWS - 1:PART:ROWS, 0, 1, :], x_rows[:, 0, 0, :]).then_inc(edge_loaded, 16)
                    else:
                        sp.dma_start(x_in[:, n.slot, :, :],
                                     x_tiles[:, bass.ds(n.times(2, -1), 2), :]).then_inc(x_loaded[n.slot], 16)
                a = s - 4
                if a.within(GROUPS):
                    sp.wait_ge(sum_done[FFN2], a.times(2 * RESIDUAL_SUMS, 2 * RESIDUAL_SUMS))
                    sp.dma_start(out_tiles[:, bass.ds(a.times(2), 2), :], y[:, a.slot, :, :]).then_inc(y_stored[a.slot], 16)

            run_steps(sp, body, FIRST_FULL, PAIRS - 5)
            for c in range(2):
                sp.wait_ge(y_stored[c], 16 * (GROUPS // 2))

        def await_x(eng, n):
            if n.reg is None and n.const in (0, PAIRS - 1):
                eng.wait_ge(edge_loaded, 96 if n.const == 0 else 192)
            else:
                eng.wait_ge(x_loaded[n.slot], n.times(8, 8 if n.slot else 0))

        @block.gpsimd
        def _(pool):
            nc.gpsimd.memset(be_raw[:], 0.0).then_inc(be_zero, 1)
            pool.wait_ge(be_zero, 1)
            for r in range(2 * 4):
                pool.dma_start(be_raw[r * E:(r + 1) * E, :], be).then_inc(small_loaded, 16)
            for k in range(KB):
                pool.dma_start(bp_col[:, k:k + 1], bp.rearrange("(k p) -> p k", p=PART)[:, k:k + 1]).then_inc(small_loaded, 16)
                pool.dma_start(wg_raw[:, k, :], Wg[k * PART:(k + 1) * PART, :]).then_inc(small_loaded, 16)
            for w, b_ in enumerate((bq, bk, bv)):
                pool.dma_start(bqkv[:, w * D:(w + 1) * D], b_.partition_broadcast(PART)).then_inc(small_loaded, 16)
            pool.dma_start(bo_all[:], bo.partition_broadcast(PART)).then_inc(small_loaded, 16)
            for t in range(2):
                pool.dma_start(bg_all[:, t, :], bg.partition_broadcast(PART)).then_inc(small_loaded, 16)
            nc.gpsimd.memset(ident[:], 0.0).then_inc(ident_set, 1)
            pool.wait_ge(ident_set, 1)
            nc.gpsimd.affine_select(out=ident[:], in_=ident[:], compare_op=ALU.not_equal, fill=1.0, base=0,
                                    pattern=[[-1, PART]], channel_multiplier=1).then_inc(ident_set, 1)
            for e in range(E):
                nc.gpsimd.memset(expert_no[:, :, :, e], float(e))
            nc.gpsimd.memset(gate_parts[:], 0.0)
            nc.gpsimd.memset(eps[:], EPS)
            nc.gpsimd.memset(minus_half[:], -0.5).then_inc(consts_set, 1)
            pool.wait_ge(consts_set, 1)

            def rstd_step(ln, n):
                pool.wait_ge(stat_done[ln], n.times(4, 4))
                await_(pool, normed_done[ln], n.times(2))
                nc.gpsimd.tensor_tensor(var_eps[:, ln, :], mean_var[:, ln, :, 1], eps[:], ALU.add).then_inc(rstd_done[ln], 1)
                pool.wait_ge(rstd_done[ln], n.times(2, 1))
                nc.gpsimd.tensor_tensor(rstd[:, ln, :], var_eps[:, ln, :], minus_half[:], ALU.pow).then_inc(rstd_done[ln], 1)

            def base_step(f, n):
                if f == FFN1:
                    await_x(pool, n)
                else:
                    pool.wait_ge(x2_done, n.times(1, 1))
                pool.wait_ge(bias_copied[f], n.times(1, 1))
                await_(pool, chain_done[f], n.times(8))
                nc.gpsimd.tensor_tensor(base[:, f], (x_in if f == FFN1 else x2)[:, n.slot], bias_sum[:, f],
                                        ALU.add).then_inc(base_done[f], 1)

            def sum_step(f, n, t):
                done, first = sum_done[f], n.times(2 * RESIDUAL_SUMS, RESIDUAL_SUMS * t)
                pool.wait_ge(chain_done[f], n.times(8, 4 * t + 4))
                pool.wait_ge(scaled_done[f], n.times(4, 2 * t + 2))
                nc.gpsimd.tensor_tensor(chain_sum[:, f, t], chain_sum[:, f, t], scaled[:, f, t, 1], ALU.add).then_inc(done, 1)
                pool.wait_ge(done, n.times(2 * RESIDUAL_SUMS, RESIDUAL_SUMS * t + 1))
                nc.gpsimd.tensor_tensor(pool_sum[:, f, t], chain_sum[:, f, t, 0], scaled[:, f, t, 0, 1], ALU.add).then_inc(done, 1)
                pool.wait_ge(done, n.times(2 * RESIDUAL_SUMS, RESIDUAL_SUMS * t + 2))
                if f == FFN1:
                    await_(pool, normed_done[LN2], (n - 1).times(2))
                else:
                    await_(pool, y_stored[n.slot], n.times(8, -8 * n.slot))
                nc.gpsimd.tensor_tensor((x1 if f == FFN1 else y)[:, n.slot, t], pool_sum[:, f, t], chain_sum[:, f, t, 1],
                                        ALU.add).then_inc(done, 1)

            def x1_bo_step(n):
                if n.reg is None and n.const == 0:
                    pool.wait_ge(setup_dve, 7)
                await_(pool, x2_done, (n - 1).times(1))
                pool.wait_ge(sum_done[FFN1], n.times(2 * RESIDUAL_SUMS, 2 * RESIDUAL_SUMS))
                nc.gpsimd.tensor_tensor(x1_bo[:, 2 * n.slot:2 * n.slot + 2, :], x1[:, n.slot],
                                        bo_all[:].unsqueeze(1).to_broadcast([PART, 2, D]), ALU.add).then_inc(x1_bo_done, 1)

            def body(s):
                if (s + 1).within(PAIRS):
                    rstd_step(LN1, s + 1)
                if s.within(PAIRS):
                    sum_step(FFN1, s, 0)
                    sum_step(FFN1, s, 1)
                    rstd_step(LN2, s)
                if (s - 4).within(GROUPS):
                    base_step(FFN2, s - 4)
                if (s - 1).within(PAIRS):
                    x1_bo_step(s - 1)
                if (s - 3).within(GROUPS):
                    rstd_step(LN3, s - 3)
                if (s - 4).within(GROUPS):
                    sum_step(FFN2, s - 4, 0)
                    sum_step(FFN2, s - 4, 1)
                if (s + 1).within(PAIRS):
                    base_step(FFN1, s + 1)

            run_steps(pool, body)

        @block.scalar
        def _(act):
            act.wait_ge(setup_pe, 1)
            for k in range(KB):
                nc.scalar.copy(wT[:, k, 0:2 * D], ffn_bank[2 * k][:, :])
                nc.scalar.copy(wT[:, k, 2 * D:3 * D], ffn_bank[2 * k + 1][:, 0:D]).then_inc(setup_act, 1)
            nc.scalar.copy(woT[:], tr_bank[0][:, :].rearrange("p (k n) -> p k n", k=KB))
            nc.scalar.copy(wo_hi[:], tr_bank[0][:, :].rearrange("p (k n) -> p k n", k=KB)).then_inc(setup_act, 1)
            act.wait_ge(small_loaded, 16 * 18)
            nc.scalar.copy(wg_hi[:], wg_raw[:])
            nc.scalar.copy(be_hi[:].bitcast(f32r), be_raw[:]).then_inc(setup_act, 1)
            act.wait_ge(setup_pe, 2)
            for k in range(KB):
                nc.scalar.copy(wqkv_hi[:, k, 0:2 * D], ffn_bank[2 * k][:, :])
                nc.scalar.copy(wqkv_hi[:, k, 2 * D:3 * D], ffn_bank[2 * k + 1][:, 0:D]).then_inc(setup_act, 1)
            act.wait_ge(we_loaded, 32)
            for k in range(KB):
                nc.scalar.copy(we_hi[:, k, :], we_raw[:, k, :]).then_inc(setup_act, 1)
            act.wait_ge(setup_pe, 4)
            nc.scalar.copy(bv_wide[:], tr_bank[1][:, 0:KB * PART].rearrange("p (k n) -> p k n", k=KB)).then_inc(setup_act, 1)

            def hi_step(i, n):
                act.wait_ge(T_done[i], n.times(1, 1))
                if i in (TA, TD):
                    await_(act, bank_full[FFN1 if i == TA else FFN2], n.times(8))
                elif i == TB:
                    await_(act, v_done, n.times(1))
                else:
                    await_(act, proj_done, n.times(1))
                nc.scalar.copy(T_hi[i][:].rearrange("p t k n -> p (t k n)"), t_bank[i][:, :]).then_inc(hi_done[i], 1)

            def second_step(f, n):
                act.wait_ge(gate_ops[f], n.times(GATE_OPS, 6))
                nc.scalar.activation(second[:, f], margin[:, f], ACT.Exp).then_inc(second_done[f], 1)

            def gateT_step(f, n):
                act.wait_ge(gateT_done[f], n.times(1, 1))
                await_(act, bias_done[f], n.times(1))
                nc.scalar.copy(gateT[:, f], gateT_bank[f][:, 0:PART]).then_inc(gateT_copied[f], 1)

            def bias_step(f, n):
                act.wait_ge(bias_done[f], n.times(1, 1))
                await_(act, base_done[f], n.times(1))
                nc.scalar.copy(bias_sum[:, f].rearrange("p t n -> p (t n)"), bias_bank[f][:, :]).then_inc(bias_copied[f], 1)

            def scale_step(f, n, t):
                act.wait_ge(gate_ops[f], n.times(GATE_OPS, 13))
                await_(act, sum_done[f], (n - 1).times(2 * RESIDUAL_SUMS, RESIDUAL_SUMS * t + 2))
                for half, b in enumerate((0, 2)):
                    act.wait_ge(bank_full[f], n.times(8, 4 * t + b + 1))
                    for j in range(2):
                        e = 2 * b + j
                        last = nc.scalar.activation(scaled[:, f, t, half, j], ffn_bank[b][:, j * D:(j + 1) * D],
                                                    ACT.Copy, scale=gate[:, f, t, e:e + 1])
                    last.then_inc(scaled_done[f], 1)

            def v_step(n):
                act.wait_ge(v_done, n.times(1, 1))
                await_(act, attn_ops, (n - 2).times(ATTN_OPS, 14))
                nc.scalar.copy(v[:, 2 * n.slot:2 * n.slot + 2, :].rearrange("p t n -> p (t n)"),
                               mix_bank[0][:, :]).then_inc(v_copied, 1)

            def exp_step(a):
                act.wait_ge(attn_ops, a.times(ATTN_OPS, 7))
                await_(act, attn_ops, (a - 1).times(ATTN_OPS, 14))
                nc.scalar.activation(prob[:], score[:], ACT.Exp, scale=DH ** -0.5).then_inc(exp_done, 1)

            def body(s):
                if s.within(PAIRS):
                    scale_step(FFN1, s, 0)
                    scale_step(FFN1, s, 1)
                if (s - 3).within(GROUPS):
                    hi_step(TO, s - 3)
                if (s + 1).within(PAIRS):
                    hi_step(TA, s + 1)
                if (s - 4).within(GROUPS):
                    second_step(FFN2, s - 4)
                if (s - 1).within(PAIRS):
                    v_step(s - 1)
                if (s - 4).within(GROUPS):
                    gateT_step(FFN2, s - 4)
                    bias_step(FFN2, s - 4)
                if (s + 1).within(PAIRS):
                    second_step(FFN1, s + 1)
                if (s - 4).within(GROUPS):
                    scale_step(FFN2, s - 4, 0)
                    scale_step(FFN2, s - 4, 1)
                if (s - 2).within(GROUPS):
                    exp_step(s - 2)
                if s.within(PAIRS):
                    hi_step(TB, s)
                if (s + 1).within(PAIRS):
                    gateT_step(FFN1, s + 1)
                if (s - 3).within(GROUPS):
                    hi_step(TD, s - 3)
                if (s + 1).within(PAIRS):
                    bias_step(FFN1, s + 1)

            run_steps(act, body)

        @block.vector
        def _(dve):
            dve.wait_ge(ident_set, 2)
            for m in range(4):
                last = nc.vector.tensor_reduce(row_mask[:, m:m + 1], ident[:, 16 * m:16 * (m + 1)], AX.X, ALU.add)
            last.then_inc(setup_dve, 1)
            dve.wait_ge(small_loaded, 16 * 18)
            dve.wait_ge(setup_act, 3)
            nc.vector.tensor_copy(bp_wide[:], bp_col[:].unsqueeze(2).to_broadcast([PART, KB, PART])).then_inc(setup_dve, 1)
            nc.vector.tensor_tensor(wo_lo[:], tr_bank[0][:, :].rearrange("p (k n) -> p k n", k=KB),
                                    wo_hi[:].bitcast(f32), ALU.subtract)
            dve.wait_ge(setup_act, 4)
            nc.vector.tensor_tensor(wg_lo[:], wg_raw[:], wg_hi[:].bitcast(f32), ALU.subtract)
            nc.vector.tensor_tensor(be_lo[:], be_raw[:], be_hi[:], ALU.subtract).then_inc(setup_dve, 1)
            dve.wait_ge(setup_dve, 3)
            for t in range(2):
                nc.vector.tensor_scalar(out=be_raw[:], in0=be_lo[:], scalar1=row_mask[:, 2 * t + 1:2 * t + 2],
                                        scalar2=None, op0=ALU.mult).then_inc(masks_set, 1)
                dve.wait_ge(masks_set, 2 * t + 1)
                nc.vector.scalar_tensor_tensor(out=be_rows[:, t, :], in0=be_hi[:], scalar=row_mask[:, 2 * t:2 * t + 1],
                                               in1=be_raw[:], op0=ALU.mult, op1=ALU.add).then_inc(masks_set, 1)
                dve.wait_ge(masks_set, 2 * t + 2)
            dve.wait_ge(setup_pe, 3)
            nc.vector.tensor_tensor(bqkv[:, 0:2 * D], mix_bank[0][:, :], bqkv[:, 0:2 * D], ALU.add)
            nc.vector.tensor_tensor(bqkv[:, 2 * D:3 * D], mix_bank[1][:, 0:D], bqkv[:, 2 * D:3 * D],
                                    ALU.add).then_inc(setup_dve, 1)
            dve.wait_ge(setup_act, 6)
            for k in range(KB):
                nc.vector.tensor_tensor(wqkv_lo[:, k, 0:2 * D], ffn_bank[2 * k][:, :],
                                        wqkv_hi[:, k, 0:2 * D].bitcast(f32), ALU.subtract)
                last = nc.vector.tensor_tensor(wqkv_lo[:, k, 2 * D:3 * D], ffn_bank[2 * k + 1][:, 0:D],
                                               wqkv_hi[:, k, 2 * D:3 * D].bitcast(f32), ALU.subtract)
            last.then_inc(setup_dve, 1)
            for k in range(KB):
                dve.wait_ge(setup_act, 7 + k)
                last = nc.vector.tensor_tensor(we_lo[:, k, :], we_raw[:, k, :], we_hi[:, k, :].bitcast(f32), ALU.subtract)
            last.then_inc(setup_dve, 1)
            dve.wait_ge(setup_pe, 5)
            nc.vector.tensor_tensor(bo_all[:], mix_bank[0][:, 0:D], bo_all[:], ALU.add).then_inc(setup_dve, 1)
            dve.wait_ge(setup_dve, 7)
            dve.wait_ge(consts_set, 1)

            def await_apart(s, value):
                dve.wait_ge(s, value)
                nc.vector.tensor_copy(idle[:], minus_half[:])

            def stats_step(ln, n):
                source = {LN1: x_in, LN2: x1, LN3: x2}[ln]
                if ln == LN1:
                    await_x(dve, n)
                for t in range(2):
                    if ln == LN2:
                        dve.wait_ge(sum_done[FFN1], n.times(2 * RESIDUAL_SUMS, RESIDUAL_SUMS * (t + 1)))
                    elif ln == LN3 and t == 0:
                        dve.wait_ge(x2_done, n.times(1, 1))
                    nc.vector.bn_stats(stats[:, ln, t], source[:, n.slot, t]).then_inc(stat_done[ln], 1)
                await_apart(stat_done[ln], n.times(4, 2))
                for t in range(2):
                    nc.vector.bn_aggr(mean_var[:, ln, t], stats[:, ln, t]).then_inc(stat_done[ln], 1)

            def normalise_step(ln, n):
                source = {LN1: x_in, LN2: x1, LN3: x2}[ln]
                dve.wait_ge(rstd_done[ln], n.times(2, 2))
                await_(dve, T_done[T_OF_LN[ln]], n.times(1))
                for t in range(2):
                    nc.vector.tensor_scalar(out=normed[:, ln, t], in0=source[:, n.slot, t],
                                            scalar1=mean_var[:, ln, t, 0:1], scalar2=rstd[:, ln, t:t + 1],
                                            op0=ALU.subtract, op1=ALU.mult).then_inc(normed_done[ln], 1)

            def lo_step(i, n):
                dve.wait_ge(hi_done[i], n.times(1, 1))
                nc.vector.tensor_tensor(T_lo[i][:].rearrange("p t k n -> p (t k n)"), t_bank[i][:, :],
                                        T_hi[i][:].rearrange("p t k n -> p (t k n)").bitcast(f32),
                                        ALU.subtract).then_inc(lo_done[i], 1)

            def gate_step(f, n):
                ops = gate_ops[f]

                def after(k):
                    dve.wait_ge(ops, n.times(GATE_OPS, k))

                dve.wait_ge(logits_done[f], n.times(1, 1))
                nc.vector.tensor_tensor(logits[:, f].rearrange("p t e -> p (t e)"), logit_bank[f][:, 0:2 * E],
                                        bg_all[:].rearrange("p t e -> p (t e)"), ALU.add).then_inc(ops, 1)
                await_apart(ops, n.times(GATE_OPS, 1))
                for t in range(2):
                    nc.vector.max(top[:, f, t], logits[:, f, t]).then_inc(ops, 1)
                await_apart(ops, n.times(GATE_OPS, 3))
                for t in range(2):
                    nc.vector.max_index(top_at[:, f, t], top[:, f, t], logits[:, f, t]).then_inc(ops, 1)
                nc.vector.tensor_tensor(margin[:, f], top[:, f, :, 1], top[:, f, :, 0], ALU.subtract).then_inc(ops, 1)
                after(5)
                nc.vector.tensor_copy(top_no[:, f], top_at[:, f, :, 0:2]).then_inc(ops, 1)
                after(7)
                nc.vector.tensor_tensor(hot[:, f], expert_no[:], top_no[:, f].unsqueeze(3).to_broadcast([PART, 2, 2, E]),
                                        ALU.is_equal).then_inc(ops, 1)
                dve.wait_ge(second_done[f], n.times(1, 1))
                nc.vector.tensor_scalar(out=twice_sum[:, f], in0=second[:, f], scalar1=1.0, scalar2=2.0,
                                        op0=ALU.add, op1=ALU.mult).then_inc(ops, 1)
                after(9)
                nc.vector.reciprocal(share[:, f, :, 0], twice_sum[:, f]).then_inc(ops, 1)
                after(10)
                nc.vector.tensor_tensor(share[:, f, :, 1], share[:, f, :, 0], second[:, f], ALU.mult).then_inc(ops, 1)
                after(11)
                nc.vector.tensor_tensor(hot_share[:, f], hot[:, f], share[:, f].unsqueeze(3).to_broadcast([PART, 2, 2, E]),
                                        ALU.mult).then_inc(ops, 1)
                after(12)
                await_(dve, scaled_done[f], n.times(4))
                nc.vector.tensor_tensor(gate[:, f], hot_share[:, f, :, 0], hot_share[:, f, :, 1], ALU.add).then_inc(ops, 1)
                after(13)
                await_(dve, gateT_done[f], n.times(1))
                nc.vector.tensor_copy(gate_parts[:, f, 0:2, 0:4:2, :].bitcast(f32r),
                                      gate[:, f].unsqueeze(2).to_broadcast([PART, 2, 2, E])).then_inc(ops, 1)
                after(14)
                nc.vector.tensor_tensor(gate_parts[:, f, 0:2, 1:4:2, :], gate[:, f].unsqueeze(2).to_broadcast([PART, 2, 2, E]),
                                        gate_parts[:, f, 0:2, 0:4:2, :], ALU.subtract).then_inc(ops, 1)

            def chain_step(f, n, t, b):
                done = chain_done[f]
                if b == 1:
                    dve.wait_ge(gate_ops[f], n.times(GATE_OPS, 13))
                    dve.wait_ge(base_done[f], n.times(1, 1))
                    dve.wait_ge(scaled_done[f], n.times(4, 2 * t + 1))
                    await_(dve, sum_done[f], (n - 1).times(2 * RESIDUAL_SUMS, RESIDUAL_SUMS * (t + 1)))
                dve.wait_ge(bank_full[f], n.times(8, 4 * t + b + 1))
                for j in range(2):
                    e = 2 * b + j
                    if b == 1:
                        start = (base[:, f, t], scaled[:, f, t, 0, 0])[j]
                    else:
                        start = chain_sum[:, f, t, j]
                        dve.wait_ge(done, n.times(8, 4 * t + 1 + j))
                    nc.vector.scalar_tensor_tensor(out=chain_sum[:, f, t, j], in0=ffn_bank[b][:, j * D:(j + 1) * D],
                                                   scalar=gate[:, f, t, e:e + 1], in1=start,
                                                   op0=ALU.mult, op1=ALU.add).then_inc(done, 1)

            def qk_step(n):
                for t in range(2):
                    dve.wait_ge(qk_done, n.times(2, t + 1))
                    nc.vector.tensor_tensor(qk[:, 2 * n.slot + t].rearrange("p w n -> p (w n)"), mix_bank[t][:, :],
                                            bqkv[:, 0:2 * D], ALU.add).then_inc(qk_copied, 1)

            def runs(slots):
                return [(0, 2, slice(slots[0], slots[0] + 2))] if slots[1] == slots[0] + 1 else \
                    [(0, 1, slice(slots[0], slots[0] + 1)), (1, 2, slice(slots[1], slots[1] + 1))]

            def slots_of(a, first):
                return [(2 * a.slot + first + i) % 4 for i in range(2)]

            def score_step(a):
                ops = attn_ops
                dve.wait_ge(qk_copied, a.times(2, 4))
                q_slots = slots_of(a, 1)
                for m in range(3):
                    k_slots = slots_of(a, m)
                    both = len(runs(q_slots)) == 1 and len(runs(k_slots)) == 1
                    if both:
                        last = nc.vector.tensor_tensor(prod[:, m], qk[:, q_slots[0]:q_slots[0] + 2, 0],
                                                       qk[:, k_slots[0]:k_slots[0] + 2, 1], ALU.mult)
                    else:
                        for t in range(2):
                            last = nc.vector.tensor_tensor(prod[:, m, t], qk[:, q_slots[t], 0], qk[:, k_slots[t], 1], ALU.mult)
                    last.then_inc(ops, 1)
                dve.wait_ge(ops, a.times(ATTN_OPS, 3))
                nc.vector.tensor_reduce(score[:].rearrange("p m h -> p (m h)"),
                                        prod[:].rearrange("p m t (h d) -> p (m t h) d", d=DH), AX.X, ALU.add).then_inc(ops, 1)

            def weights_step(a, part):
                ops = attn_ops

                def after(k):
                    dve.wait_ge(ops, a.times(ATTN_OPS, k))

                if part == 0:
                    after(4)
                    nc.vector.tensor_tensor(most[:, 0], score[:, 0], score[:, 1], ALU.max).then_inc(ops, 1)
                    after(5)
                    nc.vector.tensor_tensor(most[:, 1], most[:, 0], score[:, 2], ALU.max).then_inc(ops, 1)
                    after(6)
                    nc.vector.tensor_tensor(score[:], score[:], most[:, 1].unsqueeze(1).to_broadcast([PART, 3, 2 * H]),
                                            ALU.subtract).then_inc(ops, 1)
                else:
                    dve.wait_ge(exp_done, a.times(1, 1))
                    nc.vector.tensor_tensor(total[:, 0], prob[:, 0], prob[:, 1], ALU.add).then_inc(ops, 1)
                    after(8)
                    nc.vector.tensor_tensor(total[:, 1], total[:, 0], prob[:, 2], ALU.add).then_inc(ops, 1)
                    after(9)
                    nc.vector.reciprocal(total[:, 2], total[:, 1]).then_inc(ops, 1)
                    after(10)
                    nc.vector.tensor_tensor(prob[:], prob[:], total[:, 2].unsqueeze(1).to_broadcast([PART, 3, 2 * H]),
                                            ALU.mult).then_inc(ops, 1)

            def value_step(a):
                ops = attn_ops
                dve.wait_ge(ops, a.times(ATTN_OPS, 11))
                dve.wait_ge(v_copied, a.times(1, 2))
                for m in range(3):
                    for t0, t1, at in runs(slots_of(a, m)):
                        nt = t1 - t0
                        last = nc.vector.tensor_tensor(
                            prod[:, m, t0:t1].rearrange("p t (h d) -> p (t h) d", d=DH),
                            v[:, at].rearrange("p t (h d) -> p (t h) d", d=DH),
                            prob[:, m, t0 * H:t1 * H].unsqueeze(2).to_broadcast([PART, nt * H, DH]), ALU.mult)
                    last.then_inc(ops, 1)
                dve.wait_ge(ops, a.times(ATTN_OPS, 13))
                nc.vector.tensor_tensor(prod[:, 0], prod[:, 0], prod[:, 1], ALU.add).then_inc(ops, 1)
                dve.wait_ge(ops, a.times(ATTN_OPS, 15))
                await_(dve, T_done[TO], a.times(1))
                nc.vector.tensor_tensor(attn[:], prod[:, 0], prod[:, 2], ALU.add).then_inc(ops, 1)

            def x2_step(a):
                dve.wait_ge(proj_done, a.times(1, 1))
                dve.wait_ge(x1_bo_done, a.times(1, 2))
                await_(dve, base_done[FFN2], (a - 1).times(1))
                for t0, t1, at in runs(slots_of(a, 1)):
                    last = nc.vector.tensor_tensor(x2[:, a.slot, t0:t1].rearrange("p t n -> p (t n)"),
                                                   mix_bank[1][:, t0 * D:t1 * D],
                                                   x1_bo[:, at].rearrange("p t n -> p (t n)"), ALU.add)
                last.then_inc(x2_done, 1)

            def body(s):
                ffn1, ffn2 = s.within(PAIRS), (s - 4).within(GROUPS)
                if (s + 1).within(PAIRS):
                    stats_step(LN1, s + 1)
                if (s - 3).within(GROUPS):
                    weights_step(s - 3, 1)
                if ffn1:
                    chain_step(FFN1, s, 0, 1)
                if (s - 3).within(GROUPS):
                    value_step(s - 3)
                if ffn1:
                    chain_step(FFN1, s, 0, 3)
                if (s + 1).within(PAIRS):
                    normalise_step(LN1, s + 1)
                if ffn1:
                    chain_step(FFN1, s, 1, 1)
                    chain_step(FFN1, s, 1, 3)
                if (s - 3).within(GROUPS):
                    lo_step(TO, s - 3)
                if (s + 1).within(PAIRS):
                    lo_step(TA, s + 1)
                if ffn2:
                    gate_step(FFN2, s - 4)
                if (s - 1).within(PAIRS):
                    qk_step(s - 1)
                if s.within(PAIRS):
                    stats_step(LN2, s)
                if (s - 3).within(GROUPS):
                    x2_step(s - 3)
                    stats_step(LN3, s - 3)
                if s.within(PAIRS):
                    normalise_step(LN2, s)
                if (s + 1).within(PAIRS):
                    gate_step(FFN1, s + 1)
                if ffn2:
                    chain_step(FFN2, s - 4, 0, 1)
                if (s - 2).within(GROUPS):
                    score_step(s - 2)
                if ffn2:
                    chain_step(FFN2, s - 4, 0, 3)
                if (s - 3).within(GROUPS):
                    normalise_step(LN3, s - 3)
                if ffn2:
                    chain_step(FFN2, s - 4, 1, 1)
                if (s - 2).within(GROUPS):
                    weights_step(s - 2, 0)
                if ffn2:
                    chain_step(FFN2, s - 4, 1, 3)
                if s.within(PAIRS):
                    lo_step(TB, s)
                if (s - 3).within(GROUPS):
                    lo_step(TD, s - 3)

            run_steps(dve, body)

        @block.tensor
        def _(pe):
            pe.wait_ge(ident_set, 2)
            pe.wait_ge(w_loaded, 16 * 5)
            for w in range(3):
                for ob in range(KB):
                    for mb in range(KB):
                        bank = ffn_bank[2 * mb + (w == 2)]
                        at = (w % 2) * D + ob * PART
                        nc.tensor.transpose(bank[:, at:at + PART], w_raw[:, w, ob, mb * PART:(mb + 1) * PART], ident[:])
            for ob in range(KB):
                for mb in range(KB):
                    last = nc.tensor.transpose(tr_bank[0][:, mb * D + ob * PART:mb * D + (ob + 1) * PART],
                                               w_raw[:, 3, ob, mb * PART:(mb + 1) * PART], ident[:])
            last.then_inc(setup_pe, 1)
            pe.wait_ge(setup_act, 2)
            for db in range(KB):
                for bank, c0, c1 in ((ffn_bank[2 * db], 0, 2 * D), (ffn_bank[2 * db + 1], 2 * D, 3 * D)):
                    for mb in range(KB):
                        last = nc.tensor.matmul(bank[:, 0:c1 - c0], w_raw[:, 4, mb, db * PART:(db + 1) * PART],
                                                wT[:, mb, c0:c1], start=(mb == 0), stop=(mb == KB - 1))
            last.then_inc(setup_pe, 1)
            pe.wait_ge(setup_dve, 2)
            for bank, c0, c1 in ((mix_bank[0], 0, 2 * D), (mix_bank[1], 2 * D, 3 * D)):
                for mb in range(KB):
                    last = nc.tensor.matmul(bank[:, 0:c1 - c0], bp_wide[:, mb, :], wT[:, mb, c0:c1],
                                            start=(mb == 0), stop=(mb == KB - 1))
            last.then_inc(setup_pe, 1)
            pe.wait_ge(setup_dve, 4)
            for mb in range(KB):
                last = nc.tensor.transpose(tr_bank[1][:, mb * PART:(mb + 1) * PART],
                                           bqkv[:, 2 * D + mb * PART:2 * D + (mb + 1) * PART], ident[:])
            last.then_inc(setup_pe, 1)
            pe.wait_ge(setup_act, 9)
            for mb in range(KB):
                last = nc.tensor.matmul(mix_bank[0][:, 0:D], bv_wide[:, mb, :], woT[:, mb, :],
                                        start=(mb == 0), stop=(mb == KB - 1))
            last.then_inc(setup_pe, 1)
            pe.wait_ge(setup_dve, 7)
            pe.wait_ge(masks_set, 4)

            def product(dest, i, t, w_hi_, w_lo_, c0, c1, low_low=False):
                terms = []
                for k in range(KB):
                    terms += [(T_hi[i], w_hi_, k), (T_hi[i], w_lo_, k), (T_lo[i], w_hi_, k)]
                    if low_low:
                        terms.append((T_lo[i], w_lo_, k))
                for j, (left, right, k) in enumerate(terms):
                    last = nc.tensor.matmul(dest, left[:, t, k, :], right[:, k, c0:c1],
                                            start=(j == 0), stop=(j == len(terms) - 1))
                return last

            def T_step(i, n):
                source = attn if i == TO else normed[:, {TA: LN1, TB: LN2, TD: LN3}[i]]
                if i == TO:
                    pe.wait_ge(attn_ops, n.times(ATTN_OPS, ATTN_OPS))
                    await_(pe, lo_done[TB], min_pairs(n + 2))
                else:
                    pe.wait_ge(normed_done[{TA: LN1, TB: LN2, TD: LN3}[i]], n.times(2, 2))
                    if i == TA:
                        await_(pe, lo_done[TD], (n - 5).times(1, 1))
                    elif i == TB:
                        await_(pe, gateT_copied[FFN2], (n - 4).times(1, 1))
                    else:
                        pe.wait_ge(gate_ops[FFN1], min_pairs(n + 4, 0, GATE_OPS))
                for t in range(2):
                    for k in range(KB):
                        at = (t * KB + k) * PART
                        last = nc.tensor.transpose(t_bank[i][:, at:at + PART], source[:, t, k * PART:(k + 1) * PART], ident[:])
                last.then_inc(T_done[i], 1)

            def min_pairs(n, plus=0, per=1):
                if n.reg is None and n.const > PAIRS - 1:
                    return per * PAIRS
                return n.times(per, per) + plus

            def logits_step(f, n, s):
                i = T_OF_FFN[f]
                pe.wait_ge(lo_done[i], n.times(1, 1))
                if f == FFN2:
                    await_(pe, bias_copied[FFN1], min_pairs(s))
                for t in range(2):
                    last = product(logit_bank[f][:, t * E:(t + 1) * E], i, t, wg_hi, wg_lo, 0, E, low_low=True)
                last.then_inc(logits_done[f], 1)

            def gateT_step(f, n, s):
                pe.wait_ge(gate_ops[f], n.times(GATE_OPS, GATE_OPS))
                if f == FFN1:
                    await_(pe, bias_copied[FFN2], (s - 4).times(1, 1))
                    if s.reg is None:
                        await_(pe, v_copied, (s - 1).times(1, 1))
                else:
                    await_(pe, lo_done[TO], min_groups(s - 3))
                nc.tensor.transpose(gateT_bank[f][:, 0:PART], gate_parts[:, f].rearrange("p a b e -> p (a b e)"),
                                    ident[:]).then_inc(gateT_done[f], 1)

            def min_groups(a, per=1):
                if a.reg is None and a.const > GROUPS - 1:
                    return per * GROUPS
                return a.times(per, per)

            def bias_step(f, n, s):
                pe.wait_ge(gateT_copied[f], n.times(1, 1))
                if f == FFN1:
                    await_(pe, x2_done, (s - 3).times(1, 1))
                    if s.reg is None:
                        await_(pe, bias_copied[FFN1], n.times(1))
                        await_(pe, qk_copied, (s - 1).times(2, 2))
                else:
                    await_(pe, v_copied, min_pairs(s - 1))
                    if s.reg is None:
                        await_(pe, bias_copied[FFN2], n.times(1))
                for t in range(2):
                    last = nc.tensor.matmul(bias_bank[f][:, t * D:(t + 1) * D], gateT[:, f], be_rows[:, t, :],
                                            start=True, stop=True)
                last.then_inc(bias_done[f], 1)

            def ffn_step(f, n, s):
                i = T_OF_FFN[f]
                pe.wait_ge(lo_done[i], n.times(1, 1))
                for t in range(2):
                    for b in range(4):
                        if t == 1:
                            before = (f, n, 0)
                        elif f == FFN1:
                            before = (FFN2, s - 5, 1) if (s - 5).within(GROUPS) else (FFN1, n - 1, 1)
                        else:
                            before = (FFN1, s, 1) if s.within(PAIRS) else (FFN2, n - 1, 1)
                        g, m, u = before
                        if b % 2:
                            await_(pe, chain_done[g], m.times(8, 4 * u + b + 1))
                        else:
                            await_(pe, scaled_done[g], m.times(4, 2 * u + b // 2 + 1))
                        product(ffn_bank[b][:, :], i, t, we_hi, we_lo, b * BANK, (b + 1) * BANK).then_inc(bank_full[f], 1)

            def qkv_step(n, s):
                pe.wait_ge(lo_done[TB], n.times(1, 1))
                await_(pe, gateT_copied[FFN1], min_pairs(s))
                if s.reg is None:
                    await_(pe, bias_copied[FFN2], (s - 5).times(1, 1))
                    await_(pe, bias_copied[FFN1], min_pairs(s))
                for t in range(2):
                    if t == 1:
                        await_(pe, gate_ops[FFN2], (s - 4).times(GATE_OPS, 1))
                    product(mix_bank[t][:, :], TB, t, wqkv_hi, wqkv_lo, 0, 2 * D).then_inc(qk_done, 1)
                pe.wait_ge(qk_copied, n.times(2, 1))
                for t in range(2):
                    last = product(mix_bank[0][:, t * D:(t + 1) * D], TB, t, wqkv_hi, wqkv_lo, 2 * D, 3 * D)
                last.then_inc(v_done, 1)

            def projection_step(a, s):
                pe.wait_ge(lo_done[TO], a.times(1, 1))
                await_(pe, qk_copied, min_pairs(s - 1, 0, 2))
                for t in range(2):
                    last = product(mix_bank[1][:, t * D:(t + 1) * D], TO, t, wo_hi, wo_lo, 0, D)
                last.then_inc(proj_done, 1)

            def body(s):
                if s.within(PAIRS):
                    ffn_step(FFN1, s, s)
                if (s - 3).within(GROUPS):
                    T_step(TO, s - 3)
                if (s - 4).within(GROUPS):
                    logits_step(FFN2, s - 4, s)
                if (s + 1).within(PAIRS):
                    T_step(TA, s + 1)
                if (s - 1).within(PAIRS):
                    qkv_step(s - 1, s)
                if (s - 4).within(GROUPS):
                    gateT_step(FFN2, s - 4, s)
                if (s - 3).within(GROUPS):
                    projection_step(s - 3, s)
                if (s + 1).within(PAIRS):
                    logits_step(FFN1, s + 1, s)
                if (s - 4).within(GROUPS):
                    bias_step(FFN2, s - 4, s)
                    ffn_step(FFN2, s - 4, s)
                if s.within(PAIRS):
                    T_step(TB, s)
                if (s + 1).within(PAIRS):
                    gateT_step(FFN1, s + 1, s)
                if (s - 3).within(GROUPS):
                    T_step(TD, s - 3)
                if (s + 1).within(PAIRS):
                    bias_step(FFN1, s + 1, s)

            run_steps(pe, body)


def kernel(**inputs):
    import numpy as np
    import concourse.bacc as bacc
    from concourse.bass_utils import run_bass_kernel_spmd

    nc = bacc.Bacc("TRN2", target_bir_lowering=False, num_devices=1)
    arrays, args = {}, []
    for name in INPUTS:
        a = np.ascontiguousarray(inputs[name])
        arrays[f"in_{name}"] = a
        args.append(nc.dram_tensor(f"in_{name}", a.shape, mybir.dt.from_np(a.dtype), kind="ExternalInput").ap())
    out = nc.dram_tensor("out_x", (B, S, D), mybir.dt.float32, kind="ExternalOutput").ap()
    build(nc, *args, out)
    return run_bass_kernel_spmd(nc, [arrays], core_ids=[0]).results[0]["out_x"]
```

```python
import concourse.bass as bass
from concourse import mybir
from contextlib import ExitStack

INPUTS = ["L0_attn_x", "L0_attn_Wp", "L0_attn_bp", "L0_attn_Wq", "L0_attn_bq", "L0_attn_Wk", "L0_attn_bk",
          "L0_attn_Wv", "L0_attn_bv", "L0_attn_Wo", "L0_attn_bo", "L0_ffn_We", "L0_ffn_be", "L0_ffn_Wg", "L0_ffn_bg"]
B, S, D, H, E = 4, 2048, 256, 16, 8
DH = D // H
PART = 128
TILES = B * S // PART
ROWS = S // TILES
KB = D // PART
PAIRS = TILES // 2
GROUPS = TILES // 2
BANK = 512
EPS = 1e-5
LOWEST_STEP, FIRST_FULL, LAST_FULL, LAST_STEP = -1, 7, 28, GROUPS + 3
GATE_OPS = 14
RSTD_OPS = 4
ATTN_OPS = 16
MOVES = 3 * 2 * B
RESIDUAL_SUMS = 3


class Step:

    def __init__(self, const, reg=None):
        self.const, self.reg = const, reg

    def __add__(self, k):
        return Step(self.const + k, self.reg)

    def __sub__(self, k):
        return Step(self.const - k, self.reg)

    @property
    def slot(self):
        return self.const % 2

    def within(self, count):
        return self.reg is not None or 0 <= self.const < count

    def times(self, per, plus=0):
        value = per * self.const + plus
        return value if self.reg is None else self.reg * (2 * per) + value


def await_(eng, sem, value):
    if not isinstance(value, int) or value > 0:
        eng.wait_ge(sem, value)


def run_steps(eng, body, first_full=FIRST_FULL, last_full=LAST_FULL):
    for s in range(LOWEST_STEP, first_full):
        body(Step(s))
    with eng.Fori(0, (last_full + 1 - first_full) // 2) as i:
        for u in range(2):
            body(Step(first_full + u, i))
    for s in range(last_full + 1, LAST_STEP + 1):
        body(Step(s))


def build(nc, x, Wp, bp, Wq, bq, Wk, bk, Wv, bv, Wo, bo, We, be, Wg, bg, out):
    f32, f32r, u32 = mybir.dt.float32, mybir.dt.float32r, mybir.dt.uint32
    ACT, ALU, AX = mybir.ActivationFunctionType, mybir.AluOpType, mybir.AxisListType
    FFN1, FFN2 = 0, 1
    NF = 2
    LN1, LN2, LN3 = range(3)
    TA, TB, TO, TD = range(4)
    T_OF_LN = {LN1: TA, LN2: TB, LN3: TD}
    T_OF_FFN = {FFN1: TA, FFN2: TD}

    with ExitStack() as ctx:
        def sb(name, shape, dt=f32):
            return ctx.enter_context(nc.sbuf_tensor(name, shape, dt))

        def pb(name):
            return ctx.enter_context(nc.psum_tensor(name, [PART, BANK], f32))

        def sem(name):
            return ctx.enter_context(nc.semaphore(name))

        we_hi, we_lo = sb("we_hi", [PART, KB, E * D], f32r), sb("we_lo", [PART, KB, E * D], f32r)
        wqkv_hi, wqkv_lo = sb("wqkv_hi", [PART, KB, 3 * D], f32r), sb("wqkv_lo", [PART, KB, 3 * D], f32r)
        wo_hi, wo_lo = sb("wo_hi", [PART, KB, D], f32r), sb("wo_lo", [PART, KB, D], f32r)
        wg = sb("wg", [PART, KB, 2, E], f32r)
        be_rows = sb("be_rows", [PART, NF * 2, D], f32r)
        bqkv = sb("bqkv", [PART, 3 * D])
        bo_all = sb("bo_all", [PART, D])
        bg_all = sb("bg_all", [PART, E])
        ident = sb("ident", [PART, PART])
        expert_no = sb("expert_no", [PART, NF * 2 * 2, E])
        idle = sb("idle", [PART, 2])
        minus_half, minus_one, eps = (sb(name, [PART, 2]) for name in ("minus_half", "minus_one", "eps"))
        we_raw = sb("we_raw", [PART, KB, E * D])
        w_raw = sb("w_raw", [PART, 5, KB, D])
        wT, woT = sb("wT", [PART, KB, 3 * D]), sb("woT", [PART, KB, D])
        wg_raw = sb("wg_raw", [PART, KB, E])
        bp_col = sb("bp_col", [PART, KB])
        bp_wide, bv_wide = sb("bp_wide", [PART, KB, PART]), sb("bv_wide", [PART, KB, PART])
        be_raw, be_hi, be_lo = sb("be_raw", [PART, D]), sb("be_hi", [PART, D]), sb("be_lo", [PART, D])
        row_mask = sb("row_mask", [PART, NF * 2 * 2])
        x_in = sb("x_in", [PART, 2, 2, D])
        stats = sb("stats", [PART, 3, 2, 6])
        mean_var = sb("mean_var", [PART, 3, 2, 2])
        var_eps, rstd, minus_mean, shift = (
            sb(name, [PART, 3, 2]) for name in ("var_eps", "rstd", "minus_mean", "shift"))
        normed = sb("normed", [PART, 3, 2, D])
        T_hi = [[sb(f"T_hi{i}_{c}", [PART, 2, KB, PART], f32r) for c in range(2 if i in (TA, TD) else 1)] for i in range(4)]
        T_lo = [[sb(f"T_lo{i}_{c}", [PART, 2, KB, PART], f32r) for c in range(2 if i in (TA, TD) else 1)] for i in range(4)]
        logits = sb("logits", [PART, NF * 2, E])
        top = sb("top", [PART, NF * 2, 8])
        top_at = sb("top_at", [PART, NF * 2, 8], u32)
        top_no = sb("top_no", [PART, NF * 2, 2])
        margin, second, twice_sum = (sb(name, [PART, NF * 2]) for name in ("margin", "second", "twice_sum"))
        share = sb("share", [PART, NF * 2, 2])
        hot, hot_share = sb("hot", [PART, NF * 2, 2, E]), sb("hot_share", [PART, NF * 2, 2, E])
        gate = sb("gate", [PART, NF * 2, E])
        gate_parts = sb("gate_parts", [PART, NF * 2, 4, E])
        gateT = sb("gateT", [PART, PART], f32r)
        bias_sum = sb("bias_sum", [PART, NF, 2, D])
        base = sb("base", [PART, NF, 2, D])
        scaled = we_raw[:].rearrange("p k (a b c n) -> p k a b c n", a=2, b=2, c=2)
        chain_sum = sb("chain_sum", [PART, NF, 2, 2, D])
        pool_sum = sb("pool_sum", [PART, NF, 2, D])
        x1 = sb("x1", [PART, 2, 2, D])
        x1_bo = sb("x1_bo", [PART, 4, D])
        qk = sb("qk", [PART, 4, 2, D])
        v = sb("v", [PART, 4, D])
        moved_qk, moved_v = sb("moved_qk", [PART, 2, 2, D]), sb("moved_v", [PART, 2, D])
        moved_x1_bo = sb("moved_x1_bo", [PART, 2, D])
        prod = sb("prod", [PART, 3, 2, D])
        score, prob = sb("score", [PART, 3, 2 * H]), sb("prob", [PART, 3, 2 * H])
        most = sb("most", [PART, 2, 2 * H])
        total = sb("total", [PART, 3, 2 * H])
        attn = sb("attn", [PART, 2, D])
        x2 = sb("x2", [PART, 2, 2, D])
        y = sb("y", [PART, 2, 2, D])

        ffn_bank = [pb(f"ffn_bank{b}") for b in range(4)]
        tr_bank = [pb(f"tr_bank{b}") for b in range(2)]
        mix_bank = [pb(f"mix_bank{b}") for b in range(2)]
        t_bank = {TO: tr_bank[0], TB: tr_bank[0], TA: tr_bank[1], TD: tr_bank[1]}
        logit_bank, gateT_bank, proj_bank = tr_bank[1], tr_bank[0], tr_bank[1]
        v_bank, bias_bank = mix_bank[0], mix_bank

        w_loaded, wp_loaded = sem("w_loaded"), sem("wp_loaded")
        bp_loaded, bqkv_loaded, small_loaded = sem("bp_loaded"), sem("bqkv_loaded"), sem("small_loaded")
        we_loaded = [sem(f"we_loaded{k}") for k in range(KB)]
        consts_set, masks_set, ident_set = sem("consts_set"), sem("masks_set"), sem("ident_set")
        setup_act, setup_dve, setup_pe = sem("setup_act"), sem("setup_dve"), sem("setup_pe")
        pair_moved = sem("pair_moved")
        x_loaded = [sem(f"x_loaded{c}") for c in range(2)]
        y_stored = [sem(f"y_stored{c}") for c in range(2)]
        stat_done = [sem(f"stat_done{i}") for i in range(3)]
        rstd_done = [sem(f"rstd_done{i}") for i in range(3)]
        normed_done = [sem(f"normed_done{i}") for i in range(3)]
        T_done = [sem(f"T_done{i}") for i in range(4)]
        hi_done = [sem(f"hi_done{i}") for i in range(4)]
        lo_done = [sem(f"lo_done{i}") for i in range(4)]
        logits_done, gate_ops, second_done = sem("logits_done"), sem("gate_ops"), sem("second_done")
        gateT_done, gateT_copied = sem("gateT_done"), sem("gateT_copied")
        bias_done = [sem(f"bias_done{f}") for f in range(NF)]
        bias_copied = [sem(f"bias_copied{f}") for f in range(NF)]
        base_done = [sem(f"base_done{f}") for f in range(NF)]
        bank_full = [sem(f"bank_full{f}") for f in range(NF)]
        scaled_done = [sem(f"scaled_done{f}") for f in range(NF)]
        chain_done = [sem(f"chain_done{f}") for f in range(NF)]
        sum_done = [sem(f"sum_done{f}") for f in range(NF)]
        qk_done, v_done = sem("qk_done"), sem("v_done")
        qk_copied, v_copied = sem("qk_copied"), sem("v_copied")
        attn_ops, exp_done, proj_done, x2_done, x1_bo_done = (
            sem("attn_ops"), sem("exp_done"), sem("proj_done"), sem("x2_done"), sem("x1_bo_done"))

        block = ctx.enter_context(nc.Block())
        x_tiles = x.rearrange("b (r j) d -> (b r) j d", j=TILES)
        out_tiles = out.rearrange("b (r j) d -> (b r) j d", j=TILES)
        out_rows = out.rearrange("b (r j) d -> b r j d", j=TILES)

        def gates_of(s):
            return slice(0 if (s + 1).within(PAIRS) else 2, 4 if (s - 4).within(GROUPS) else 2)

        def gate_round(f, n):
            return n if f == FFN1 else n + 5

        @block.sync
        def _(sp):
            for w, W in enumerate((Wq, Wk, Wv, Wo, Wp)):
                sp.dma_start(w_raw[:, w, :, :], W.rearrange("(k p) n -> p k n", p=PART)).then_inc(
                    w_loaded if w < 4 else wp_loaded, 16)
            for n in range(2):
                sp.dma_start(x_in[:, n, :, :], x_tiles[:, 2 * n:2 * n + 2, :]).then_inc(x_loaded[n], 16)
            for k in range(KB):
                sp.dma_start(we_raw[:, k, :].rearrange("p (e n) -> p e n", e=E),
                             We[:, k * PART:(k + 1) * PART, :].rearrange("e p n -> p e n")).then_inc(we_loaded[k], 16)

            def body(s):
                n = s + 3
                if n.within(PAIRS):
                    await_(sp, base_done[FFN1], (s + 1).times(1, 1))
                    sp.dma_start(x_in[:, n.slot, :, :], x_tiles[:, bass.ds(n.times(2), 2), :]).then_inc(x_loaded[n.slot], 16)
                if s.reg is None and s.const == 1:
                    for moved, source, done, value in ((moved_qk[:], qk[:, 0:2], qk_copied, 2),
                                                       (moved_v[:], v[:, 0:2], v_copied, 1),
                                                       (moved_x1_bo[:], x1_bo[:, 0:2], x1_bo_done, 1)):
                        sp.wait_ge(done, value)
                        for b in range(B):
                            sp.dma_start(moved[ROWS * b:ROWS * (b + 1) - 1],
                                         source[ROWS * b + 1:ROWS * (b + 1)]).then_inc(pair_moved, 16)
                            sp.dma_start(moved[ROWS * (b + 1) - 1:ROWS * (b + 1)],
                                         source[ROWS * b:ROWS * b + 1]).then_inc(pair_moved, 16)
                a = s - 4
                if a.within(GROUPS):
                    sp.wait_ge(sum_done[FFN2], a.times(2 * RESIDUAL_SUMS, 2 * RESIDUAL_SUMS))
                    if a.reg is None and a.const == GROUPS - 1:
                        sp.dma_start(out_tiles[:, TILES - 1, :], y[:, a.slot, 0, :]).then_inc(y_stored[a.slot], 16)
                        for b in range(B):
                            sp.dma_start(out_rows[b, 1:ROWS, 0, :],
                                         y[ROWS * b:ROWS * (b + 1) - 1, a.slot, 1, :]).then_inc(y_stored[a.slot], 16)
                        sp.dma_start(out_rows[:, 0, 0, :], y[ROWS - 1:PART:ROWS, a.slot, 1, :]).then_inc(y_stored[a.slot], 16)
                    else:
                        sp.dma_start(out_tiles[:, bass.ds(a.times(2, 1), 2), :], y[:, a.slot, :, :]).then_inc(y_stored[a.slot], 16)

            run_steps(sp, body)
            sp.wait_ge(y_stored[0], 16 * (GROUPS // 2))
            sp.wait_ge(y_stored[1], 16 * (GROUPS // 2 + B + 1))

        def halves(i, n):
            return (T_hi[i][n.slot], T_lo[i][n.slot]) if i in (TA, TD) else (T_hi[i][0], T_lo[i][0])

        def await_x(eng, n):
            eng.wait_ge(x_loaded[n.slot], n.times(8, 8 if n.slot else 16))

        @block.gpsimd
        def _(pool):
            nc.gpsimd.memset(ident[:], 0.0).then_inc(ident_set, 1)
            pool.wait_ge(ident_set, 1)
            nc.gpsimd.affine_select(out=ident[:], in_=ident[:], compare_op=ALU.not_equal, fill=1.0, base=0,
                                    pattern=[[-1, PART]], channel_multiplier=1).then_inc(ident_set, 1)
            for e in range(E):
                nc.gpsimd.memset(expert_no[:, :, e], float(e))
            nc.gpsimd.memset(gate_parts[:], 0.0)
            nc.gpsimd.memset(eps[:], EPS)
            nc.gpsimd.memset(minus_one[:], -1.0)
            nc.gpsimd.memset(minus_half[:], -0.5).then_inc(consts_set, 1)
            for k in range(KB):
                pool.dma_start(bp_col[:, k:k + 1], bp.rearrange("(k p) -> p k", p=PART)[:, k:k + 1]).then_inc(bp_loaded, 16)
            for w, b_ in enumerate((bq, bk, bv)):
                pool.dma_start(bqkv[:, w * D:(w + 1) * D], b_.partition_broadcast(PART)).then_inc(bqkv_loaded, 16)
            pool.dma_start(wg_raw[:], Wg.rearrange("(k p) e -> p k e", p=PART)).then_inc(small_loaded, 16)
            pool.dma_start(be_raw[:], be.partition_broadcast(PART // E)).then_inc(small_loaded, 16)
            pool.dma_start(bg_all[:], bg.partition_broadcast(PART)).then_inc(small_loaded, 16)
            pool.dma_start(bo_all[:], bo.partition_broadcast(PART)).then_inc(small_loaded, 16)
            pool.wait_ge(consts_set, 1)

            def rstd_step(ln, n):
                done = rstd_done[ln]

                def after(k):
                    pool.wait_ge(done, n.times(RSTD_OPS, k))

                pool.wait_ge(stat_done[ln], n.times(4, 4))
                await_(pool, normed_done[ln], n.times(2))
                nc.gpsimd.tensor_tensor(var_eps[:, ln], mean_var[:, ln, :, 1], eps[:], ALU.add).then_inc(done, 1)
                nc.gpsimd.tensor_tensor(minus_mean[:, ln], mean_var[:, ln, :, 0], minus_one[:], ALU.mult).then_inc(done, 1)
                after(1)
                nc.gpsimd.tensor_tensor(rstd[:, ln], var_eps[:, ln], minus_half[:], ALU.pow).then_inc(done, 1)
                after(3)
                nc.gpsimd.tensor_tensor(shift[:, ln], minus_mean[:, ln], rstd[:, ln], ALU.mult).then_inc(done, 1)

            def base_step(f, n):
                if f == FFN1:
                    await_x(pool, n)
                else:
                    pool.wait_ge(x2_done, n.times(1, 1))
                pool.wait_ge(bias_copied[f], n.times(1, 1))
                await_(pool, chain_done[f], n.times(8))
                nc.gpsimd.tensor_tensor(base[:, f], (x_in if f == FFN1 else x2)[:, n.slot], bias_sum[:, f],
                                        ALU.add).then_inc(base_done[f], 1)

            def sum_step(f, n, t):
                done, first = sum_done[f], n.times(2 * RESIDUAL_SUMS, RESIDUAL_SUMS * t)
                pool.wait_ge(chain_done[f], n.times(8, 4 * t + 4))
                pool.wait_ge(scaled_done[f], n.times(4, 2 * t + 2))
                nc.gpsimd.tensor_tensor(chain_sum[:, f, t], chain_sum[:, f, t], scaled[:, f, t, 1], ALU.add).then_inc(done, 1)
                pool.wait_ge(done, n.times(2 * RESIDUAL_SUMS, RESIDUAL_SUMS * t + 1))
                nc.gpsimd.tensor_tensor(pool_sum[:, f, t], chain_sum[:, f, t, 0], scaled[:, f, t, 0, 1], ALU.add).then_inc(done, 1)
                pool.wait_ge(done, n.times(2 * RESIDUAL_SUMS, RESIDUAL_SUMS * t + 2))
                if f == FFN1:
                    await_(pool, normed_done[LN2], (n - 1).times(2))
                else:
                    await_(pool, y_stored[n.slot], n.times(8, -8 * n.slot))
                nc.gpsimd.tensor_tensor((x1 if f == FFN1 else y)[:, n.slot, t], pool_sum[:, f, t], chain_sum[:, f, t, 1],
                                        ALU.add).then_inc(done, 1)

            def x1_bo_step(n):
                if n.reg is None and n.const == 0:
                    pool.wait_ge(setup_dve, 7)
                await_(pool, x2_done, (n - 1).times(1))
                if n.reg is None and n.const in (2, PAIRS):
                    pool.wait_ge(pair_moved, 16 * MOVES)
                if n.reg is None and n.const == PAIRS:
                    nc.gpsimd.tensor_copy(x1_bo[:, 0:2, :], moved_x1_bo[:]).then_inc(x1_bo_done, 1)
                    return
                pool.wait_ge(sum_done[FFN1], n.times(2 * RESIDUAL_SUMS, 2 * RESIDUAL_SUMS))
                nc.gpsimd.tensor_tensor(x1_bo[:, 2 * n.slot:2 * n.slot + 2, :], x1[:, n.slot],
                                        bo_all[:].unsqueeze(1).to_broadcast([PART, 2, D]), ALU.add).then_inc(x1_bo_done, 1)

            rstd_step(LN1, Step(0))

            def body(s):
                if s.within(PAIRS):
                    sum_step(FFN1, s, 0)
                    sum_step(FFN1, s, 1)
                    rstd_step(LN2, s)
                if (s - 4).within(GROUPS):
                    base_step(FFN2, s - 4)
                if (s - 3).within(GROUPS):
                    rstd_step(LN3, s - 3)
                if (s - 1).within(PAIRS + 1):
                    x1_bo_step(s - 1)
                if (s + 2).within(PAIRS):
                    rstd_step(LN1, s + 2)
                if (s - 4).within(GROUPS):
                    sum_step(FFN2, s - 4, 0)
                    sum_step(FFN2, s - 4, 1)
                if (s + 1).within(PAIRS):
                    base_step(FFN1, s + 1)

            run_steps(pool, body)

        @block.scalar
        def _(act):
            act.wait_ge(setup_pe, 1)
            for k in range(KB):
                nc.scalar.copy(wT[:, k, 0:2 * D], ffn_bank[2 * k][:, :])
                nc.scalar.copy(wT[:, k, 2 * D:3 * D], ffn_bank[2 * k + 1][:, 0:D]).then_inc(setup_act, 1)
            nc.scalar.copy(woT[:], tr_bank[0][:, :].rearrange("p (k n) -> p k n", k=KB))
            nc.scalar.copy(wo_hi[:], tr_bank[0][:, :].rearrange("p (k n) -> p k n", k=KB)).then_inc(setup_act, 1)

            def hi_step(i, n):
                act.wait_ge(T_done[i], n.times(1, 1))
                if i in (TA, TD):
                    await_(act, bank_full[FFN1 if i == TA else FFN2], (n - 1).times(8))
                elif i == TB:
                    await_(act, v_done, n.times(1))
                else:
                    await_(act, proj_done, n.times(1))
                nc.scalar.copy(halves(i, n)[0][:].rearrange("p t k n -> p (t k n)"), t_bank[i][:, :]).then_inc(hi_done[i], 1)

            def second_step(g, cs):
                act.wait_ge(gate_ops, g.times(GATE_OPS, 5))
                nc.scalar.activation(second[:, cs], margin[:, cs], ACT.Exp).then_inc(second_done, 1)

            def gateT_step(g):
                act.wait_ge(gateT_done, g.times(1, 1))
                await_(act, bias_done[FFN1], min(g.const, PAIRS) if g.reg is None else g.times(1))
                await_(act, bias_done[FFN2], (g - 5).times(1))
                nc.scalar.copy(gateT[:], gateT_bank[:, 0:PART]).then_inc(gateT_copied, 1)

            def normalise_step(ln, n):
                source = {LN1: x_in, LN2: x1, LN3: x2}[ln]
                act.wait_ge(rstd_done[ln], n.times(RSTD_OPS, RSTD_OPS))
                await_(act, T_done[T_OF_LN[ln]], n.times(1))
                for t in range(2):
                    nc.scalar.activation(normed[:, ln, t], source[:, n.slot, t], ACT.Identity,
                                         scale=rstd[:, ln, t:t + 1], bias=shift[:, ln, t:t + 1]).then_inc(normed_done[ln], 1)

            def bias_step(f, n):
                act.wait_ge(bias_done[f], n.times(1, 1))
                await_(act, base_done[f], n.times(1))
                nc.scalar.copy(bias_sum[:, f].rearrange("p t n -> p (t n)"), bias_bank[f][:, :]).then_inc(bias_copied[f], 1)

            def scale_step(f, n, t):
                act.wait_ge(gate_ops, gate_round(f, n).times(GATE_OPS, 12))
                await_(act, sum_done[f], (n - 1).times(2 * RESIDUAL_SUMS, RESIDUAL_SUMS * t + 2))
                for half, b in enumerate((0, 2)):
                    act.wait_ge(bank_full[f], n.times(8, 4 * t + b + 1))
                    for j in range(2):
                        e = 2 * b + j
                        last = nc.scalar.activation(scaled[:, f, t, half, j], ffn_bank[b][:, j * D:(j + 1) * D],
                                                    ACT.Copy, scale=gate[:, 2 * f + t, e:e + 1])
                    last.then_inc(scaled_done[f], 1)

            def v_step(n):
                await_(act, attn_ops, (n - 2).times(ATTN_OPS, 14))
                if n.reg is None and n.const in (2, PAIRS):
                    act.wait_ge(pair_moved, 16 * MOVES)
                if n.reg is None and n.const == PAIRS:
                    nc.scalar.copy(v[:, 0:2, :], moved_v[:]).then_inc(v_copied, 1)
                    return
                act.wait_ge(v_done, n.times(1, 1))
                nc.scalar.copy(v[:, 2 * n.slot:2 * n.slot + 2, :].rearrange("p t n -> p (t n)"),
                               mix_bank[0][:, :]).then_inc(v_copied, 1)

            def exp_step(a):
                act.wait_ge(attn_ops, a.times(ATTN_OPS, 7))
                await_(act, attn_ops, (a - 1).times(ATTN_OPS, 14))
                nc.scalar.activation(prob[:], score[:], ACT.Exp, scale=DH ** -0.5).then_inc(exp_done, 1)

            normalise_step(LN1, Step(0))
            for k in range(KB):
                act.wait_ge(we_loaded[k], 16)
                nc.scalar.copy(we_hi[:, k, :], we_raw[:, k, :]).then_inc(setup_act, 1)
            act.wait_ge(small_loaded, 16 * 4)
            nc.scalar.copy(wg[:, :, 0], wg_raw[:])
            nc.scalar.copy(be_hi[:].bitcast(f32r), be_raw[:]).then_inc(setup_act, 1)
            act.wait_ge(setup_pe, 2)
            for k in range(KB):
                nc.scalar.copy(wqkv_hi[:, k, 0:2 * D], ffn_bank[2 * k][:, :])
                nc.scalar.copy(wqkv_hi[:, k, 2 * D:3 * D], ffn_bank[2 * k + 1][:, 0:D]).then_inc(setup_act, 1)
            hi_step(TA, Step(0))
            act.wait_ge(setup_pe, 4)
            nc.scalar.copy(bv_wide[:], tr_bank[0][:, 0:KB * PART].rearrange("p (k n) -> p k n", k=KB)).then_inc(setup_act, 1)

            def body(s):
                ffn1, ffn2 = s.within(PAIRS), (s - 4).within(GROUPS)
                filling = s.reg is None and s.const < 4
                if s.const >= 0 and (s + 1).within(PAIRS):
                    normalise_step(LN1, s + 1)
                if ffn1:
                    scale_step(FFN1, s, 0)
                if s.const >= 0 and (s + 1).within(PAIRS):
                    hi_step(TA, s + 1)
                if s.reg is None and 1 <= s.const <= 4:
                    hi_step(TB, s - 1)
                if ffn1:
                    scale_step(FFN1, s, 1)
                if (s - 3).within(GROUPS):
                    hi_step(TO, s - 3)
                second_step(s + 1, gates_of(s))
                if (s - 1).within(PAIRS + 1):
                    v_step(s - 1)
                gateT_step(s + 1)
                if ffn2:
                    bias_step(FFN2, s - 4)
                if (s + 1).within(PAIRS):
                    bias_step(FFN1, s + 1)
                if s.within(PAIRS):
                    normalise_step(LN2, s)
                if ffn2:
                    scale_step(FFN2, s - 4, 0)
                if (s - 3).within(GROUPS):
                    normalise_step(LN3, s - 3)
                if (s - 2).within(GROUPS):
                    exp_step(s - 2)
                if (s - 3).within(GROUPS):
                    hi_step(TD, s - 3)
                if ffn2:
                    scale_step(FFN2, s - 4, 1)
                if ffn1 and not filling:
                    hi_step(TB, s)

            run_steps(act, body)

        @block.vector
        def _(dve):
            def await_apart(s, value):
                dve.wait_ge(s, value)
                nc.vector.tensor_copy(idle[:], minus_half[:])

            def stats_step(ln, n):
                source = {LN1: x_in, LN2: x1, LN3: x2}[ln]
                if ln == LN1:
                    await_x(dve, n)
                for t in range(2):
                    if ln == LN2:
                        dve.wait_ge(sum_done[FFN1], n.times(2 * RESIDUAL_SUMS, RESIDUAL_SUMS * (t + 1)))
                    elif ln == LN3 and t == 0:
                        dve.wait_ge(x2_done, n.times(1, 1))
                    if t == 0:
                        await_(dve, rstd_done[ln], n.times(RSTD_OPS))
                    nc.vector.bn_stats(stats[:, ln, t], source[:, n.slot, t]).then_inc(stat_done[ln], 1)
                await_apart(stat_done[ln], n.times(4, 2))
                for t in range(2):
                    nc.vector.bn_aggr(mean_var[:, ln, t], stats[:, ln, t]).then_inc(stat_done[ln], 1)

            def lo_step(i, n):
                dve.wait_ge(hi_done[i], n.times(1, 1))
                hi, lo = halves(i, n)
                nc.vector.tensor_tensor(lo[:].rearrange("p t k n -> p (t k n)"), t_bank[i][:, :],
                                        hi[:].rearrange("p t k n -> p (t k n)").bitcast(f32),
                                        ALU.subtract).then_inc(lo_done[i], 1)

            def gate_step(g, cs, part):
                ops, nf = gate_ops, cs.stop - cs.start

                def after(k):
                    dve.wait_ge(ops, g.times(GATE_OPS, k))

                if part == 0:
                    bank = logit_bank[:, 0:NF * 2 * 2 * E].rearrange("p (c w e) -> p c w e", w=2, e=E)
                    dve.wait_ge(logits_done, g.times(1, 1))
                    nc.vector.tensor_tensor(logits[:, cs], bank[:, cs, 0], bg_all[:].unsqueeze(1).to_broadcast([PART, nf, E]),
                                            ALU.add).then_inc(ops, 1)
                    after(1)
                    nc.vector.tensor_tensor(logits[:, cs], bank[:, cs, 1], logits[:, cs], ALU.add).then_inc(ops, 1)
                    await_apart(ops, g.times(GATE_OPS, 2))
                    for c in range(cs.start, cs.stop):
                        last = nc.vector.max(top[:, c], logits[:, c])
                    last.then_inc(ops, 1)
                    await_apart(ops, g.times(GATE_OPS, 3))
                    for c in range(cs.start, cs.stop):
                        last = nc.vector.max_index(top_at[:, c], top[:, c], logits[:, c])
                    last.then_inc(ops, 1)
                    nc.vector.tensor_tensor(margin[:, cs], top[:, cs, 1], top[:, cs, 0], ALU.subtract).then_inc(ops, 1)
                    after(4)
                    nc.vector.tensor_copy(top_no[:, cs], top_at[:, cs, 0:2]).then_inc(ops, 1)
                elif part == 1:
                    after(6)
                    nc.vector.tensor_tensor(hot[:, cs].rearrange("p c k e -> p (c k) e"), expert_no[:, 0:2 * nf],
                                            top_no[:, cs].rearrange("p c k -> p (c k)").unsqueeze(2).to_broadcast([PART, 2 * nf, E]),
                                            ALU.is_equal).then_inc(ops, 1)
                    dve.wait_ge(second_done, g.times(1, 1))
                    nc.vector.tensor_scalar(out=twice_sum[:, cs], in0=second[:, cs], scalar1=1.0, scalar2=2.0,
                                            op0=ALU.add, op1=ALU.mult).then_inc(ops, 1)
                    after(8)
                    nc.vector.reciprocal(share[:, cs, 0], twice_sum[:, cs]).then_inc(ops, 1)
                    after(9)
                    nc.vector.tensor_tensor(share[:, cs, 1], share[:, cs, 0], second[:, cs], ALU.mult).then_inc(ops, 1)
                    after(10)
                    nc.vector.tensor_tensor(hot_share[:, cs].rearrange("p c k e -> p (c k) e"),
                                            hot[:, cs].rearrange("p c k e -> p (c k) e"),
                                            share[:, cs].rearrange("p c k -> p (c k)").unsqueeze(2).to_broadcast([PART, 2 * nf, E]),
                                            ALU.mult).then_inc(ops, 1)
                else:
                    after(11)
                    await_(dve, scaled_done[FFN1], min(4 * g.const, 4 * PAIRS) if g.reg is None else g.times(4))
                    await_(dve, scaled_done[FFN2], (g - 5).times(4))
                    nc.vector.tensor_tensor(gate[:, cs], hot_share[:, cs, 0], hot_share[:, cs, 1], ALU.add).then_inc(ops, 1)
                    after(12)
                    await_(dve, gateT_done, g.times(1))
                    nc.vector.tensor_copy(gate_parts[:, cs, 0:4:2, :].bitcast(f32r),
                                          gate[:, cs].unsqueeze(2).to_broadcast([PART, nf, 2, E])).then_inc(ops, 1)
                    after(13)
                    nc.vector.tensor_tensor(gate_parts[:, cs, 1:4:2, :], gate[:, cs].unsqueeze(2).to_broadcast([PART, nf, 2, E]),
                                            gate_parts[:, cs, 0:4:2, :], ALU.subtract).then_inc(ops, 1)

            def chain_step(f, n, t, b):
                done = chain_done[f]
                if b == 1:
                    dve.wait_ge(gate_ops, gate_round(f, n).times(GATE_OPS, 12))
                    dve.wait_ge(base_done[f], n.times(1, 1))
                    dve.wait_ge(scaled_done[f], n.times(4, 2 * t + 1))
                    await_(dve, sum_done[f], (n - 1).times(2 * RESIDUAL_SUMS, RESIDUAL_SUMS * (t + 1)))
                dve.wait_ge(bank_full[f], n.times(8, 4 * t + b + 1))
                for j in range(2):
                    e = 2 * b + j
                    if b == 1:
                        start = (base[:, f, t], scaled[:, f, t, 0, 0])[j]
                    else:
                        start = chain_sum[:, f, t, j]
                        dve.wait_ge(done, n.times(8, 4 * t + 1 + j))
                    nc.vector.scalar_tensor_tensor(out=chain_sum[:, f, t, j], in0=ffn_bank[b][:, j * D:(j + 1) * D],
                                                   scalar=gate[:, 2 * f + t, e:e + 1], in1=start,
                                                   op0=ALU.mult, op1=ALU.add).then_inc(done, 1)

            def qk_step(n, t):
                if n.reg is None and n.const in (2, PAIRS):
                    dve.wait_ge(pair_moved, 16 * MOVES)
                if n.reg is None and n.const == PAIRS:
                    nc.vector.tensor_copy(qk[:, t], moved_qk[:, t]).then_inc(qk_copied, 1)
                    return
                dve.wait_ge(qk_done, n.times(2, t + 1))
                nc.vector.tensor_tensor(qk[:, 2 * n.slot + t].rearrange("p w n -> p (w n)"), mix_bank[t][:, :],
                                        bqkv[:, 0:2 * D], ALU.add).then_inc(qk_copied, 1)

            def runs(slots):
                return [(0, 2, slice(slots[0], slots[0] + 2))] if slots[1] == slots[0] + 1 else \
                    [(0, 1, slice(slots[0], slots[0] + 1)), (1, 2, slice(slots[1], slots[1] + 1))]

            def slots_of(a, first):
                return [(2 * a.slot + first + i) % 4 for i in range(2)]

            def score_step(a):
                ops = attn_ops
                dve.wait_ge(qk_copied, a.times(2, 4))
                q_slots = slots_of(a, 1)
                for m in range(3):
                    k_slots = slots_of(a, m)
                    both = len(runs(q_slots)) == 1 and len(runs(k_slots)) == 1
                    if both:
                        last = nc.vector.tensor_tensor(prod[:, m], qk[:, q_slots[0]:q_slots[0] + 2, 0],
                                                       qk[:, k_slots[0]:k_slots[0] + 2, 1], ALU.mult)
                    else:
                        for t in range(2):
                            last = nc.vector.tensor_tensor(prod[:, m, t], qk[:, q_slots[t], 0], qk[:, k_slots[t], 1], ALU.mult)
                    last.then_inc(ops, 1)

            def score_sum_step(a):
                ops = attn_ops
                dve.wait_ge(ops, a.times(ATTN_OPS, 3))
                nc.vector.tensor_reduce(score[:].rearrange("p m h -> p (m h)"),
                                        prod[:].rearrange("p m t (h d) -> p (m t h) d", d=DH), AX.X, ALU.add).then_inc(ops, 1)

            def weights_step(a, part):
                ops = attn_ops

                def after(k):
                    dve.wait_ge(ops, a.times(ATTN_OPS, k))

                if part == 0:
                    after(4)
                    nc.vector.tensor_tensor(most[:, 0], score[:, 0], score[:, 1], ALU.max).then_inc(ops, 1)
                    after(5)
                    nc.vector.tensor_tensor(most[:, 1], most[:, 0], score[:, 2], ALU.max).then_inc(ops, 1)
                    after(6)
                    nc.vector.tensor_tensor(score[:], score[:], most[:, 1].unsqueeze(1).to_broadcast([PART, 3, 2 * H]),
                                            ALU.subtract).then_inc(ops, 1)
                else:
                    dve.wait_ge(exp_done, a.times(1, 1))
                    nc.vector.tensor_tensor(total[:, 0], prob[:, 0], prob[:, 1], ALU.add).then_inc(ops, 1)
                    after(8)
                    nc.vector.tensor_tensor(total[:, 1], total[:, 0], prob[:, 2], ALU.add).then_inc(ops, 1)
                    after(9)
                    nc.vector.reciprocal(total[:, 2], total[:, 1]).then_inc(ops, 1)
                    after(10)
                    nc.vector.tensor_tensor(prob[:], prob[:], total[:, 2].unsqueeze(1).to_broadcast([PART, 3, 2 * H]),
                                            ALU.mult).then_inc(ops, 1)

            def value_step(a):
                ops = attn_ops
                dve.wait_ge(ops, a.times(ATTN_OPS, 11))
                dve.wait_ge(v_copied, a.times(1, 2))
                for m in range(3):
                    for t0, t1, at in runs(slots_of(a, m)):
                        nt = t1 - t0
                        last = nc.vector.tensor_tensor(
                            prod[:, m, t0:t1].rearrange("p t (h d) -> p (t h) d", d=DH),
                            v[:, at].rearrange("p t (h d) -> p (t h) d", d=DH),
                            prob[:, m, t0 * H:t1 * H].unsqueeze(2).to_broadcast([PART, nt * H, DH]), ALU.mult)
                    last.then_inc(ops, 1)

            def value_sum_step(a):
                ops = attn_ops
                dve.wait_ge(ops, a.times(ATTN_OPS, 13))
                nc.vector.tensor_tensor(prod[:, 0], prod[:, 0], prod[:, 1], ALU.add).then_inc(ops, 1)
                dve.wait_ge(ops, a.times(ATTN_OPS, 15))
                await_(dve, T_done[TO], a.times(1))
                nc.vector.tensor_tensor(attn[:], prod[:, 0], prod[:, 2], ALU.add).then_inc(ops, 1)

            def x2_step(a):
                dve.wait_ge(proj_done, a.times(1, 1))
                dve.wait_ge(x1_bo_done, a.times(1, 2))
                await_(dve, base_done[FFN2], (a - 1).times(1))
                for t0, t1, at in runs(slots_of(a, 1)):
                    last = nc.vector.tensor_tensor(x2[:, a.slot, t0:t1].rearrange("p t n -> p (t n)"),
                                                   proj_bank[:, t0 * D:t1 * D],
                                                   x1_bo[:, at].rearrange("p t n -> p (t n)"), ALU.add)
                last.then_inc(x2_done, 1)

            dve.wait_ge(ident_set, 2)
            for m in range(NF * 2 * 2):
                last = nc.vector.tensor_reduce(row_mask[:, m:m + 1], ident[:, 16 * m:16 * (m + 1)], AX.X, ALU.add)
            last.then_inc(setup_dve, 1)
            dve.wait_ge(consts_set, 1)
            stats_step(LN1, Step(0))
            dve.wait_ge(bp_loaded, 16 * KB)
            nc.vector.tensor_copy(bp_wide[:], bp_col[:].unsqueeze(2).to_broadcast([PART, KB, PART])).then_inc(setup_dve, 1)
            dve.wait_ge(setup_act, 3)
            nc.vector.tensor_tensor(wo_lo[:], tr_bank[0][:, :].rearrange("p (k n) -> p k n", k=KB),
                                    wo_hi[:].bitcast(f32), ALU.subtract)
            dve.wait_ge(setup_act, 4)
            nc.vector.tensor_tensor(we_lo[:, 0, :], we_raw[:, 0, :], we_hi[:, 0, :].bitcast(f32), ALU.subtract)
            dve.wait_ge(setup_act, 6)
            nc.vector.tensor_tensor(wg[:, :, 1], wg_raw[:], wg[:, :, 0].bitcast(f32), ALU.subtract)
            nc.vector.tensor_tensor(be_lo[:], be_raw[:], be_hi[:], ALU.subtract).then_inc(setup_dve, 1)
            nc.vector.tensor_tensor(we_lo[:, 1, :], we_raw[:, 1, :], we_hi[:, 1, :].bitcast(f32),
                                    ALU.subtract).then_inc(setup_dve, 1)
            dve.wait_ge(setup_act, 8)
            for k in range(KB):
                nc.vector.tensor_tensor(wqkv_lo[:, k, 0:2 * D], ffn_bank[2 * k][:, :],
                                        wqkv_hi[:, k, 0:2 * D].bitcast(f32), ALU.subtract)
                last = nc.vector.tensor_tensor(wqkv_lo[:, k, 2 * D:3 * D], ffn_bank[2 * k + 1][:, 0:D],
                                               wqkv_hi[:, k, 2 * D:3 * D].bitcast(f32), ALU.subtract)
            last.then_inc(setup_dve, 1)
            dve.wait_ge(setup_pe, 3)
            dve.wait_ge(bqkv_loaded, 16 * 3)
            nc.vector.tensor_tensor(bqkv[:, 0:2 * D], mix_bank[0][:, :], bqkv[:, 0:2 * D], ALU.add)
            nc.vector.tensor_tensor(bqkv[:, 2 * D:3 * D], mix_bank[1][:, 0:D], bqkv[:, 2 * D:3 * D],
                                    ALU.add).then_inc(setup_dve, 1)
            lo_step(TA, Step(0))
            dve.wait_ge(setup_pe, 5)
            dve.wait_ge(small_loaded, 16 * 4)
            nc.vector.tensor_tensor(bo_all[:], mix_bank[0][:, 0:D], bo_all[:], ALU.add).then_inc(setup_dve, 1)
            dve.wait_ge(setup_dve, 3)
            for t in range(NF * 2):
                nc.vector.tensor_scalar(out=be_raw[:], in0=be_lo[:], scalar1=row_mask[:, 2 * t + 1:2 * t + 2],
                                        scalar2=None, op0=ALU.mult).then_inc(masks_set, 1)
                dve.wait_ge(masks_set, 2 * t + 1)
                nc.vector.scalar_tensor_tensor(out=be_rows[:, t, :], in0=be_hi[:], scalar=row_mask[:, 2 * t:2 * t + 1],
                                               in1=be_raw[:], op0=ALU.mult, op1=ALU.add).then_inc(masks_set, 1)
                dve.wait_ge(masks_set, 2 * t + 2)
            dve.wait_ge(setup_dve, 7)

            def body(s):
                ffn1, ffn2 = s.within(PAIRS), (s - 4).within(GROUPS)
                filling = s.reg is None and s.const < 4
                drains = s.reg is None and s.const >= PAIRS - 1
                drained = s.reg is None and s.const >= PAIRS
                if (s - 3).within(GROUPS) and not drained:
                    weights_step(s - 3, 1)
                if ffn1:
                    chain_step(FFN1, s, 0, 1)
                if (s - 3).within(GROUPS) and not drained:
                    value_step(s - 3)
                if ffn1:
                    chain_step(FFN1, s, 0, 3)
                if s.const >= 0 and (s + 1).within(PAIRS):
                    lo_step(TA, s + 1)
                if s.reg is None and 1 <= s.const <= 4:
                    lo_step(TB, s - 1)
                if (s - 3).within(GROUPS) and not drained:
                    value_sum_step(s - 3)
                if ffn1:
                    chain_step(FFN1, s, 1, 1)
                    chain_step(FFN1, s, 1, 3)
                gate_step(s + 1, gates_of(s), 0)
                if (s - 3).within(GROUPS):
                    lo_step(TO, s - 3)
                if (s - 1).within(PAIRS + 1):
                    qk_step(s - 1, 0)
                gate_step(s + 1, gates_of(s), 1)
                if (s - 1).within(PAIRS + 1):
                    qk_step(s - 1, 1)
                gate_step(s + 1, gates_of(s), 2)
                if s.within(PAIRS):
                    stats_step(LN2, s)
                if (s - 3).within(GROUPS):
                    x2_step(s - 3)
                    stats_step(LN3, s - 3)
                if (s + 2).within(PAIRS):
                    stats_step(LN1, s + 2)
                if (s - 2).within(GROUPS):
                    score_step(s - 2)
                if ffn2:
                    chain_step(FFN2, s - 4, 0, 1)
                if (s - 2).within(GROUPS):
                    score_sum_step(s - 2)
                if ffn2:
                    chain_step(FFN2, s - 4, 0, 3)
                if (s - 2).within(GROUPS):
                    weights_step(s - 2, 0)
                if (s - 3).within(GROUPS):
                    lo_step(TD, s - 3)
                if ffn2:
                    chain_step(FFN2, s - 4, 1, 1)
                if (s - 2).within(GROUPS) and drains:
                    weights_step(s - 2, 1)
                    value_step(s - 2)
                    value_sum_step(s - 2)
                if ffn2:
                    chain_step(FFN2, s - 4, 1, 3)
                if ffn1 and not filling:
                    lo_step(TB, s)

            run_steps(dve, body)

        @block.tensor
        def _(pe):
            pe.wait_ge(ident_set, 2)
            pe.wait_ge(w_loaded, 16 * 4)
            for w in range(3):
                for ob in range(KB):
                    for mb in range(KB):
                        bank = ffn_bank[2 * mb + (w == 2)]
                        at = (w % 2) * D + ob * PART
                        nc.tensor.transpose(bank[:, at:at + PART], w_raw[:, w, ob, mb * PART:(mb + 1) * PART], ident[:])
            for ob in range(KB):
                for mb in range(KB):
                    last = nc.tensor.transpose(tr_bank[0][:, mb * D + ob * PART:mb * D + (ob + 1) * PART],
                                               w_raw[:, 3, ob, mb * PART:(mb + 1) * PART], ident[:])
            last.then_inc(setup_pe, 1)
            pe.wait_ge(setup_act, 2)
            pe.wait_ge(wp_loaded, 16)
            for db in range(KB):
                for bank, c0, c1 in ((ffn_bank[2 * db], 0, 2 * D), (ffn_bank[2 * db + 1], 2 * D, 3 * D)):
                    for mb in range(KB):
                        last = nc.tensor.matmul(bank[:, 0:c1 - c0], w_raw[:, 4, mb, db * PART:(db + 1) * PART],
                                                wT[:, mb, c0:c1], start=(mb == 0), stop=(mb == KB - 1))
            last.then_inc(setup_pe, 1)

            def product(dest, i, n, t, w_hi_, w_lo_, c0, c1):
                hi, lo = halves(i, n)
                for k in range(KB):
                    nc.tensor.matmul(dest, hi[:, t, k, :], w_hi_[:, k, c0:c1], start=(k == 0), stop=False)
                    nc.tensor.matmul(dest, hi[:, t, k, :], w_lo_[:, k, c0:c1], start=False, stop=False)
                    last = nc.tensor.matmul(dest, lo[:, t, k, :], w_hi_[:, k, c0:c1], start=False, stop=(k == KB - 1))
                return last

            def after_pair(n, per=1):
                return per * PAIRS if n.reg is None and n.const >= PAIRS else n.times(per, per)

            def after_group(a, per=1):
                return per * GROUPS if a.reg is None and a.const >= GROUPS else a.times(per, per)

            def T_step(i, n, s):
                source = attn if i == TO else normed[:, {TA: LN1, TB: LN2, TD: LN3}[i]]
                if i == TO:
                    pe.wait_ge(attn_ops, n.times(ATTN_OPS, ATTN_OPS))
                    await_(pe, lo_done[TB], after_pair(s - 1))
                else:
                    pe.wait_ge(normed_done[{TA: LN1, TB: LN2, TD: LN3}[i]], n.times(2, 2))
                    if i == TA:
                        await_(pe, lo_done[TD], (s - 4).times(1, 1))
                    elif i == TB:
                        pe.wait_ge(gateT_copied, (s + 1).times(1, 1))
                    else:
                        pe.wait_ge(x2_done, (s - 3).times(1, 1))
                for t in range(2):
                    for k in range(KB):
                        at = (t * KB + k) * PART
                        last = nc.tensor.transpose(t_bank[i][:, at:at + PART], source[:, t, k * PART:(k + 1) * PART], ident[:])
                last.then_inc(T_done[i], 1)

            def logits_step(s):
                for c in range(gates_of(s).start, gates_of(s).stop):
                    i, t = T_OF_FFN[c // 2], c % 2
                    n = s + 1 if i == TA else s - 4
                    if t == 0:
                        pe.wait_ge(lo_done[i], n.times(1, 1))
                    for j, (T, k) in enumerate((T, k) for T in halves(i, n) for k in range(KB)):
                        last = nc.tensor.matmul(logit_bank[:, 2 * E * c:2 * E * (c + 1)], T[:, t, k, :],
                                                wg[:, k].rearrange("p w e -> p (w e)"), start=(j == 0), stop=(j == 3))
                last.then_inc(logits_done, 1)

            def gateT_step(s):
                pe.wait_ge(gate_ops, (s + 1).times(GATE_OPS, GATE_OPS))
                await_(pe, lo_done[TO], after_group(s - 3))
                if s.reg is None:
                    await_(pe, lo_done[TB], after_pair(s - 1))
                nc.tensor.transpose(gateT_bank[:, 0:PART], gate_parts[:].rearrange("p c k e -> p (c k e)"),
                                    ident[:]).then_inc(gateT_done, 1)

            def bias_step(f, s):
                if s.reg is None and s.const == -1:
                    pe.wait_ge(setup_dve, 7)
                    pe.wait_ge(masks_set, 2 * NF * 2)
                pe.wait_ge(gateT_copied, (s + 1).times(1, 1))
                if f == FFN1:
                    await_(pe, v_copied, (s - 1).times(1, 1))
                else:
                    await_(pe, qk_copied, after_pair(s - 1, 2))
                if s.reg is None:
                    await_(pe, bias_copied[f], (s + 1 if f == FFN1 else s - 4).times(1))
                for t in range(2):
                    last = nc.tensor.matmul(bias_bank[f][:, t * D:(t + 1) * D], gateT[:], be_rows[:, 2 * f + t, :],
                                            start=True, stop=True)
                last.then_inc(bias_done[f], 1)

            def ffn_step(f, n, s, t, banks=range(4)):
                i = T_OF_FFN[f]
                pe.wait_ge(lo_done[i], n.times(1, 1))
                for b in banks:
                    if t == 1:
                        before = (f, n, 0)
                    elif f == FFN1:
                        before = (FFN2, s - 5, 1) if (s - 5).within(GROUPS) else (FFN1, n - 1, 1)
                    else:
                        before = (FFN1, s, 1) if s.within(PAIRS) else (FFN2, n - 1, 1)
                    g, m, u = before
                    if b % 2:
                        await_(pe, chain_done[g], m.times(8, 4 * u + b + 1))
                    else:
                        await_(pe, scaled_done[g], m.times(4, 2 * u + b // 2 + 1))
                    product(ffn_bank[b][:, :], i, n, t, we_hi, we_lo, b * BANK, (b + 1) * BANK).then_inc(bank_full[f], 1)

            def qk_step(n, s, t):
                if t == 0:
                    pe.wait_ge(lo_done[TB], n.times(1, 1))
                if t == 0:
                    await_(pe, bias_copied[FFN1], after_pair(s))
                else:
                    await_(pe, bias_copied[FFN2], (s - 4).times(1))
                if s.reg is None:
                    await_(pe, qk_copied, (n - 1).times(2, 2))
                    await_(pe, v_copied, n.times(1))
                product(mix_bank[t][:, :], TB, n, t, wqkv_hi, wqkv_lo, 0, 2 * D).then_inc(qk_done, 1)

            def v_step(n):
                pe.wait_ge(qk_copied, n.times(2, 1))
                for t in range(2):
                    last = product(v_bank[:, t * D:(t + 1) * D], TB, n, t, wqkv_hi, wqkv_lo, 2 * D, 3 * D)
                last.then_inc(v_done, 1)

            def projection_step(a, s):
                pe.wait_ge(lo_done[TO], a.times(1, 1))
                pe.wait_ge(gate_ops, (s + 1).times(GATE_OPS, 2))
                for t in range(2):
                    last = product(proj_bank[:, t * D:(t + 1) * D], TO, a, t, wo_hi, wo_lo, 0, D)
                last.then_inc(proj_done, 1)

            T_step(TA, Step(0), Step(-1))
            pe.wait_ge(setup_dve, 2)
            for bank, c0, c1 in ((mix_bank[0], 0, 2 * D), (mix_bank[1], 2 * D, 3 * D)):
                for mb in range(KB):
                    last = nc.tensor.matmul(bank[:, 0:c1 - c0], bp_wide[:, mb, :], wT[:, mb, c0:c1],
                                            start=(mb == 0), stop=(mb == KB - 1))
            last.then_inc(setup_pe, 1)
            pe.wait_ge(setup_dve, 6)
            for mb in range(KB):
                last = nc.tensor.transpose(tr_bank[0][:, mb * PART:(mb + 1) * PART],
                                           bqkv[:, 2 * D + mb * PART:2 * D + (mb + 1) * PART], ident[:])
            last.then_inc(setup_pe, 1)
            pe.wait_ge(setup_act, 9)
            for mb in range(KB):
                last = nc.tensor.matmul(mix_bank[0][:, 0:D], bv_wide[:, mb, :], woT[:, mb, :],
                                        start=(mb == 0), stop=(mb == KB - 1))
            last.then_inc(setup_pe, 1)


            def body(s):
                filling = s.reg is None and s.const < 4
                drained = s.reg is None and s.const >= PAIRS
                if s.within(PAIRS):
                    ffn_step(FFN1, s, s, 0, range(2 if s.reg is None and s.const <= 4 else 0, 4))
                if s.const >= 0 and (s + 1).within(PAIRS):
                    T_step(TA, s + 1, s)
                if s.reg is None and 1 <= s.const <= 4:
                    T_step(TB, s - 1, s - 1)
                if s.within(PAIRS):
                    ffn_step(FFN1, s, s, 1)
                logits_step(s)
                if drained:
                    ffn_step(FFN2, s - 4, s, 0, range(0, 2))
                if (s - 3).within(GROUPS):
                    T_step(TO, s - 3, s)
                if (s - 1).within(PAIRS):
                    qk_step(s - 1, s, 0)
                    qk_step(s - 1, s, 1)
                    v_step(s - 1)
                if drained:
                    ffn_step(FFN2, s - 4, s, 0, range(2, 3))
                if (s - 3).within(GROUPS):
                    projection_step(s - 3, s)
                if filling:
                    ffn_step(FFN1, s + 1, s + 1, 0, range(0, 2))
                gateT_step(s)
                if (s - 4).within(GROUPS):
                    if not drained:
                        ffn_step(FFN2, s - 4, s, 0, range(0, 1))
                    bias_step(FFN2, s)
                    if drained:
                        ffn_step(FFN2, s - 4, s, 0, range(3, 4))
                if (s + 1).within(PAIRS):
                    bias_step(FFN1, s)
                if (s - 4).within(GROUPS):
                    if not drained:
                        ffn_step(FFN2, s - 4, s, 0, range(1, 4))
                    ffn_step(FFN2, s - 4, s, 1, range(0, 2 if drained else 1))
                if (s - 3).within(GROUPS):
                    T_step(TD, s - 3, s)
                if (s - 4).within(GROUPS):
                    ffn_step(FFN2, s - 4, s, 1, range(2 if drained else 1, 4))
                if s.within(PAIRS) and not filling:
                    T_step(TB, s, s)

            run_steps(pe, body)


def kernel(**inputs):
    import numpy as np
    import concourse.bacc as bacc
    from concourse.bass_utils import run_bass_kernel_spmd

    nc = bacc.Bacc("TRN2", target_bir_lowering=False, num_devices=1)
    arrays, args = {}, []
    for name in INPUTS:
        a = np.ascontiguousarray(inputs[name])
        arrays[f"in_{name}"] = a
        args.append(nc.dram_tensor(f"in_{name}", a.shape, mybir.dt.from_np(a.dtype), kind="ExternalInput").ap())
    out = nc.dram_tensor("out_x", (B, S, D), mybir.dt.float32, kind="ExternalOutput").ap()
    build(nc, *args, out)
    return run_bass_kernel_spmd(nc, [arrays], core_ids=[0]).results[0]["out_x"]
```
